# Optimizing a Trainium2 kernel written in Bass

```python
import numpy as np
import jax
import jax.numpy as jnp

def _softmax(x, axis=-1):
    return jax.nn.softmax(x, axis=axis)

def _gelu(x):
    return jax.nn.gelu(x, approximate=True)

def _silu(x):
    return jax.nn.silu(x)

def _sigmoid(x):
    return jax.nn.sigmoid(x)

def _layernorm(x, axis=-1, eps=1e-05):
    m = jnp.mean(x, axis=axis, keepdims=True)
    v = jnp.var(x, axis=axis, keepdims=True)
    return (x - m) / jnp.sqrt(v + eps)

def _scatter_add(tgt, idx, src, axis=0):
    return tgt.at[idx].add(src)

def _segment_sum(src, seg, n):
    return jax.ops.segment_sum(src, seg, n)
kernel_name = 'mk_gnn_resnorm_d4_gnn_r16_25b86b'

def setup_inputs(seed: int=0):
    np.random.seed(seed)
    _w = jnp.asarray

    def _rec_inputs():
        import jax
        import jax.numpy as jnp
        _gk = jax.random.key(seed)
        x = -0.000202 + 1 * jax.random.normal(jax.random.fold_in(_gk, 1), (6250, 64), jnp.float32)
        src = jax.random.randint(jax.random.fold_in(_gk, 2), (200000,), 0, 6250, jnp.int32)
        dst = jax.random.randint(jax.random.fold_in(_gk, 3), (200000,), 0, 6250, jnp.int32)
        _o = jnp.argsort(dst, stable=True)
        src = src[_o]
        dst = dst[_o]
        edge_attr_64 = -5.16925e-05 + 1.00005 * jax.random.normal(jax.random.fold_in(_gk, 11), (200000, 64), jnp.float32)
        edge_type_8 = jax.random.randint(jax.random.fold_in(_gk, 13), (200000,), 0, 8, jnp.int32)
        return (x, src, dst, edge_attr_64, edge_type_8)
    x, src, dst, edge_attr_64, edge_type_8 = _rec_inputs()

    def _L0_gnn_setup():
        import jax, jax.numpy as jnp
        import numpy as np
        N = 6250
        E = 100000
        D = 64
        NEG_SLOPE = 0.2
        EPS_IN = 1e-05

        def _instance_norm(h):
            mu = h.mean(-1, keepdims=True)
            var = ((h - mu) ** 2).mean(-1, keepdims=True)
            return (h - mu) * jax.lax.rsqrt(var + EPS_IN)

        def _gatv2(x, src, dst, edge_attr, Wl, bl, Wr, br, We, att, bo):
            xl = x @ Wl.T + bl
            xr = x @ Wr.T + br
            e = edge_attr @ We.T
            m = xl[src] + xr[dst] + e
            score = jnp.where(m > 0, m, NEG_SLOPE * m) @ att
            smax = jax.ops.segment_max(score, dst, num_segments=N)
            smax = jnp.where(jnp.isfinite(smax), smax, 0.0)
            es = jnp.exp(score - smax[dst])
            denom = jax.ops.segment_sum(es, dst, num_segments=N)
            alpha = es / (denom[dst] + 1e-16)
            out = jax.ops.segment_sum(alpha[:, None] * xl[src], dst, num_segments=N)
            return out + bo
        key = jax.random.key(seed)
        ks = jax.random.split(key, 24)
        s = 0.05
        p = lambda k, shape: jax.random.normal(k, shape, jnp.float32) * s
        inp = {'x': jax.random.normal(ks[0], (N, D), jnp.float32), 'edge_index': jax.random.randint(ks[1], (2, E), 0, N, dtype=jnp.int64), 'edge_attr': jax.random.normal(ks[2], (E, D), jnp.float32), 'Wl1': p(ks[3], (D, D)), 'bl1': p(ks[4], (D,)), 'Wr1': p(ks[5], (D, D)), 'br1': p(ks[6], (D,)), 'We1': p(ks[7], (D, D)), 'att1': p(ks[8], (D,)), 'bo1': p(ks[9], (D,)), 'Wl2': p(ks[10], (D, D)), 'bl2': p(ks[11], (D,)), 'Wr2': p(ks[12], (D, D)), 'br2': p(ks[13], (D,)), 'We2': p(ks[14], (D, D)), 'att2': p(ks[15], (D,)), 'bo2': p(ks[16], (D,)), 'Wskip': p(ks[17], (D, D)), 'bskip': p(ks[18], (D,))}
        return inp
    _L0_gnn_all = _L0_gnn_setup()
    _L0_gnn_in = {k: v for k, v in _L0_gnn_all.items() if k in ('Wl1', 'bl1', 'Wr1', 'br1', 'We1', 'att1', 'bo1', 'Wl2', 'bl2', 'Wr2', 'br2', 'We2', 'att2', 'bo2', 'Wskip', 'bskip')}
    del _L0_gnn_all

    def _L1_gnn_setup():
        import jax, jax.numpy as jnp
        import numpy as np
        N, E = (6250, 62500)
        IN_DIM, OUT_DIM, HEADS = (64, 64, 4)
        C = OUT_DIM // HEADS
        NEG_SLOPE = 0.2
        SOFTMAX_EPS = 1e-16
        LN_EPS = 1e-05

        def _gat_forward(x, edge_index, W, att_src, att_dst, bias, gamma, beta):
            src, dst = (edge_index[0], edge_index[1])
            h = (x @ W).reshape(N, HEADS, C)
            a_src = jnp.einsum('nhc,hc->nh', h, att_src)
            a_dst = jnp.einsum('nhc,hc->nh', h, att_dst)
            e = a_src[src] + a_dst[dst]
            e = jnp.where(e >= 0, e, NEG_SLOPE * e)
            m = jax.ops.segment_max(e, dst, num_segments=N)
            m = jnp.where(jnp.isfinite(m), m, 0.0)
            ex = jnp.exp(e - m[dst])
            denom = jax.ops.segment_sum(ex, dst, num_segments=N)
            alpha = ex / (denom[dst] + SOFTMAX_EPS)
            msg = alpha[:, :, None] * h[src]
            out = jax.ops.segment_sum(msg, dst, num_segments=N)
            out = out.reshape(N, HEADS * C) + bias
            mu = out.mean(axis=-1, keepdims=True)
            var = out.var(axis=-1, keepdims=True)
            out = (out - mu) * jax.lax.rsqrt(var + LN_EPS) * gamma + beta
            return out
        key = jax.random.key(seed)
        ks = jax.random.split(key, 8)
        node_input = jax.random.normal(ks[0], (N, IN_DIM), dtype=jnp.float32)
        edge_index = jax.random.randint(ks[1], (2, E), 0, N, dtype=jnp.int64)
        W = jax.random.normal(ks[2], (IN_DIM, HEADS * C), dtype=jnp.float32) / np.sqrt(IN_DIM)
        att_src = jax.random.normal(ks[3], (HEADS, C), dtype=jnp.float32) / np.sqrt(C)
        att_dst = jax.random.normal(ks[4], (HEADS, C), dtype=jnp.float32) / np.sqrt(C)
        bias = jnp.zeros((HEADS * C,), dtype=jnp.float32)
        gamma = jnp.ones((OUT_DIM,), dtype=jnp.float32)
        beta = jnp.zeros((OUT_DIM,), dtype=jnp.float32)
        return {'node_input': node_input, 'edge_index': edge_index, 'W': W, 'att_src': att_src, 'att_dst': att_dst, 'bias': bias, 'gamma': gamma, 'beta': beta}
    _L1_gnn_all = _L1_gnn_setup()
    _L1_gnn_in = {k: v for k, v in _L1_gnn_all.items() if k in ('W', 'att_src', 'att_dst', 'bias', 'gamma', 'beta')}
    del _L1_gnn_all

    def _L2_gnn_setup():
        import jax, jax.numpy as jnp
        import numpy as np
        N_NODES = 3125
        N_EDGES = 50000
        IN_DIM = 64
        OUT_DIM = 64
        N_REL = 8
        N_RULES = 32
        N_ACTIVE = 4
        LN_EPS = 1e-05

        def _seg_softmax(scores, seg, num_segments):
            m = jax.ops.segment_max(scores, seg, num_segments=num_segments)
            e = jnp.exp(scores - m[seg])
            d = jax.ops.segment_sum(e, seg, num_segments=num_segments)
            return e / d[seg]
        key = jax.random.key(seed)
        ks = jax.random.split(key, 12)
        x = jax.random.normal(ks[0], (N_NODES, IN_DIM), dtype=jnp.float32)
        edge_index = jax.random.randint(ks[1], (2, N_EDGES), 0, N_NODES, dtype=jnp.int64)
        edge_type = jax.random.randint(ks[2], (N_EDGES,), 0, N_REL, dtype=jnp.int64)
        rule_ids = jax.random.randint(ks[3], (N_ACTIVE,), 0, N_RULES, dtype=jnp.int64)
        W_r = jax.random.normal(ks[4], (N_REL, IN_DIM, OUT_DIM), dtype=jnp.float32) * (2.0 / (IN_DIM + OUT_DIM)) ** 0.5
        Wq_w = jax.random.normal(ks[5], (IN_DIM, OUT_DIM), dtype=jnp.float32) * (1.0 / IN_DIM) ** 0.5
        Wq_bias = jnp.zeros((OUT_DIM,), dtype=jnp.float32)
        Wk_w = jax.random.normal(ks[6], (3 * IN_DIM, OUT_DIM), dtype=jnp.float32) * (1.0 / (3 * IN_DIM)) ** 0.5
        Wk_bias = jnp.zeros((OUT_DIM,), dtype=jnp.float32)
        rule_emb = jax.random.normal(ks[7], (N_RULES, IN_DIM), dtype=jnp.float32) * (2.0 / (N_RULES + IN_DIM)) ** 0.5
        bias = jnp.zeros((OUT_DIM,), dtype=jnp.float32)
        ln_g = jnp.ones((OUT_DIM,), dtype=jnp.float32)
        ln_b = jnp.zeros((OUT_DIM,), dtype=jnp.float32)
        return {'x': x, 'edge_index': edge_index, 'edge_type': edge_type, 'rule_ids': rule_ids, 'W_r': W_r, 'Wq_w': Wq_w, 'Wq_bias': Wq_bias, 'Wk_w': Wk_w, 'Wk_bias': Wk_bias, 'rule_emb': rule_emb, 'bias': bias, 'ln_g': ln_g, 'ln_b': ln_b}
    _L2_gnn_all = _L2_gnn_setup()
    _L2_gnn_in = {k: v for k, v in _L2_gnn_all.items() if k in ('rule_ids', 'W_r', 'Wq_w', 'Wq_bias', 'Wk_w', 'Wk_bias', 'rule_emb', 'bias', 'ln_g', 'ln_b')}
    del _L2_gnn_all

    def _L3_gnn_setup():
        import jax, jax.numpy as jnp
        import numpy as np
        N, E, HID, NH, HD, NET = (3125, 50000, 64, 4, 16, 8)

        def _layer_norm(x, g, b, eps=1e-05):
            m = jnp.mean(x, axis=-1, keepdims=True)
            v = jnp.mean((x - m) ** 2, axis=-1, keepdims=True)
            return (x - m) * jax.lax.rsqrt(v + eps) * g + b
        key = jax.random.key(seed)
        ks = jax.random.split(key, 32)
        rn = lambda k, shape, s=0.05: jax.random.normal(k, shape, jnp.float32) * s
        return {'node_embeddings': jax.random.normal(ks[0], (N, HID), jnp.float32), 'edge_index': jax.random.randint(ks[1], (2, E), 0, N), 'edge_type': jax.random.randint(ks[2], (E,), 0, NET), 'task_embedding': jax.random.normal(ks[3], (HID,), jnp.float32), 'Wq': rn(ks[4], (HID, HID)), 'bq': jnp.zeros((HID,), jnp.float32), 'Wk': rn(ks[5], (HID, HID)), 'bk': jnp.zeros((HID,), jnp.float32), 'Wv': rn(ks[6], (HID, HID)), 'bv': jnp.zeros((HID,), jnp.float32), 'ek_tab': rn(ks[7], (NET, HID)), 'ev_tab': rn(ks[8], (NET, HID)), 'es_tab': rn(ks[9], (NET, NH)), 'eg_tab': jnp.exp(rn(ks[10], (NET, NH), 0.1)), 'Wo': rn(ks[11], (HID, HID)), 'bo': jnp.zeros((HID,), jnp.float32), 'ln1_g': jnp.ones((HID,), jnp.float32), 'ln1_b': jnp.zeros((HID,), jnp.float32), 'W1': rn(ks[12], (HID, 2 * HID)), 'b1': jnp.zeros((2 * HID,), jnp.float32), 'W2': rn(ks[13], (2 * HID, HID)), 'b2': jnp.zeros((HID,), jnp.float32), 'ln2_g': jnp.ones((HID,), jnp.float32), 'ln2_b': jnp.zeros((HID,), jnp.float32), 'Wf': rn(ks[14], (HID, 2 * HID)), 'bf': jnp.zeros((2 * HID,), jnp.float32)}
    _L3_gnn_all = _L3_gnn_setup()
    _L3_gnn_in = {k: v for k, v in _L3_gnn_all.items() if k in ('task_embedding', 'Wq', 'bq', 'Wk', 'bk', 'Wv', 'bv', 'ek_tab', 'ev_tab', 'es_tab', 'eg_tab', 'Wo', 'bo', 'ln1_g', 'ln1_b', 'W1', 'b1', 'W2', 'b2', 'ln2_g', 'ln2_b', 'Wf', 'bf')}
    del _L3_gnn_all
    return {'x': x, 'src': src, 'dst': dst, 'edge_attr_64': edge_attr_64, 'edge_type_8': edge_type_8, 'L0_gnn_Wl1': _L0_gnn_in['Wl1'], 'L0_gnn_bl1': _L0_gnn_in['bl1'], 'L0_gnn_Wr1': _L0_gnn_in['Wr1'], 'L0_gnn_br1': _L0_gnn_in['br1'], 'L0_gnn_We1': _L0_gnn_in['We1'], 'L0_gnn_att1': _L0_gnn_in['att1'], 'L0_gnn_bo1': _L0_gnn_in['bo1'], 'L0_gnn_Wl2': _L0_gnn_in['Wl2'], 'L0_gnn_bl2': _L0_gnn_in['bl2'], 'L0_gnn_Wr2': _L0_gnn_in['Wr2'], 'L0_gnn_br2': _L0_gnn_in['br2'], 'L0_gnn_We2': _L0_gnn_in['We2'], 'L0_gnn_att2': _L0_gnn_in['att2'], 'L0_gnn_bo2': _L0_gnn_in['bo2'], 'L0_gnn_Wskip': _L0_gnn_in['Wskip'], 'L0_gnn_bskip': _L0_gnn_in['bskip'], 'L1_gnn_W': _L1_gnn_in['W'], 'L1_gnn_att_src': _L1_gnn_in['att_src'], 'L1_gnn_att_dst': _L1_gnn_in['att_dst'], 'L1_gnn_bias': _L1_gnn_in['bias'], 'L1_gnn_gamma': _L1_gnn_in['gamma'], 'L1_gnn_beta': _L1_gnn_in['beta'], 'L2_gnn_rule_ids': _L2_gnn_in['rule_ids'], 'L2_gnn_W_r': _L2_gnn_in['W_r'], 'L2_gnn_Wq_w': _L2_gnn_in['Wq_w'], 'L2_gnn_Wq_bias': _L2_gnn_in['Wq_bias'], 'L2_gnn_Wk_w': _L2_gnn_in['Wk_w'], 'L2_gnn_Wk_bias': _L2_gnn_in['Wk_bias'], 'L2_gnn_rule_emb': _L2_gnn_in['rule_emb'], 'L2_gnn_bias': _L2_gnn_in['bias'], 'L2_gnn_ln_g': _L2_gnn_in['ln_g'], 'L2_gnn_ln_b': _L2_gnn_in['ln_b'], 'L3_gnn_task_embedding': _L3_gnn_in['task_embedding'], 'L3_gnn_Wq': _L3_gnn_in['Wq'], 'L3_gnn_bq': _L3_gnn_in['bq'], 'L3_gnn_Wk': _L3_gnn_in['Wk'], 'L3_gnn_bk': _L3_gnn_in['bk'], 'L3_gnn_Wv': _L3_gnn_in['Wv'], 'L3_gnn_bv': _L3_gnn_in['bv'], 'L3_gnn_ek_tab': _L3_gnn_in['ek_tab'], 'L3_gnn_ev_tab': _L3_gnn_in['ev_tab'], 'L3_gnn_es_tab': _L3_gnn_in['es_tab'], 'L3_gnn_eg_tab': _L3_gnn_in['eg_tab'], 'L3_gnn_Wo': _L3_gnn_in['Wo'], 'L3_gnn_bo': _L3_gnn_in['bo'], 'L3_gnn_ln1_g': _L3_gnn_in['ln1_g'], 'L3_gnn_ln1_b': _L3_gnn_in['ln1_b'], 'L3_gnn_W1': _L3_gnn_in['W1'], 'L3_gnn_b1': _L3_gnn_in['b1'], 'L3_gnn_W2': _L3_gnn_in['W2'], 'L3_gnn_b2': _L3_gnn_in['b2'], 'L3_gnn_ln2_g': _L3_gnn_in['ln2_g'], 'L3_gnn_ln2_b': _L3_gnn_in['ln2_b'], 'L3_gnn_Wf': _L3_gnn_in['Wf'], 'L3_gnn_bf': _L3_gnn_in['bf']}

def reference(x, src, dst, edge_attr_64, edge_type_8, L0_gnn_Wl1, L0_gnn_bl1, L0_gnn_Wr1, L0_gnn_br1, L0_gnn_We1, L0_gnn_att1, L0_gnn_bo1, L0_gnn_Wl2, L0_gnn_bl2, L0_gnn_Wr2, L0_gnn_br2, L0_gnn_We2, L0_gnn_att2, L0_gnn_bo2, L0_gnn_Wskip, L0_gnn_bskip, L1_gnn_W, L1_gnn_att_src, L1_gnn_att_dst, L1_gnn_bias, L1_gnn_gamma, L1_gnn_beta, L2_gnn_rule_ids, L2_gnn_W_r, L2_gnn_Wq_w, L2_gnn_Wq_bias, L2_gnn_Wk_w, L2_gnn_Wk_bias, L2_gnn_rule_emb, L2_gnn_bias, L2_gnn_ln_g, L2_gnn_ln_b, L3_gnn_task_embedding, L3_gnn_Wq, L3_gnn_bq, L3_gnn_Wk, L3_gnn_bk, L3_gnn_Wv, L3_gnn_bv, L3_gnn_ek_tab, L3_gnn_ev_tab, L3_gnn_es_tab, L3_gnn_eg_tab, L3_gnn_Wo, L3_gnn_bo, L3_gnn_ln1_g, L3_gnn_ln1_b, L3_gnn_W1, L3_gnn_b1, L3_gnn_W2, L3_gnn_b2, L3_gnn_ln2_g, L3_gnn_ln2_b, L3_gnn_Wf, L3_gnn_bf):
    import jax
    import jax.numpy as jnp

    def _L0_gnn_ref(x, edge_index, edge_attr, Wl1, bl1, Wr1, br1, We1, att1, bo1, Wl2, bl2, Wr2, br2, We2, att2, bo2, Wskip, bskip):
        import jax, jax.numpy as jnp
        import numpy as np
        N = 6250
        E = 100000
        D = 64
        NEG_SLOPE = 0.2
        EPS_IN = 1e-05

        def _instance_norm(h):
            mu = h.mean(-1, keepdims=True)
            var = ((h - mu) ** 2).mean(-1, keepdims=True)
            return (h - mu) * jax.lax.rsqrt(var + EPS_IN)

        def _gatv2(x, src, dst, edge_attr, Wl, bl, Wr, br, We, att, bo):
            xl = x @ Wl.T + bl
            xr = x @ Wr.T + br
            e = edge_attr @ We.T
            m = xl[src] + xr[dst] + e
            score = jnp.where(m > 0, m, NEG_SLOPE * m) @ att
            smax = jax.ops.segment_max(score, dst, num_segments=N)
            smax = jnp.where(jnp.isfinite(smax), smax, 0.0)
            es = jnp.exp(score - smax[dst])
            denom = jax.ops.segment_sum(es, dst, num_segments=N)
            alpha = es / (denom[dst] + 1e-16)
            out = jax.ops.segment_sum(alpha[:, None] * xl[src], dst, num_segments=N)
            return out + bo
        src, dst = (edge_index[0], edge_index[1])
        h = jax.nn.relu(_gatv2(x, src, dst, edge_attr, Wl1, bl1, Wr1, br1, We1, att1, bo1))
        h = _instance_norm(h)
        h2 = jax.nn.relu(_gatv2(h, src, dst, edge_attr, Wl2, bl2, Wr2, br2, We2, att2, bo2) + x @ Wskip.T + bskip)
        return _instance_norm(h2)

    def _L1_gnn_ref(node_input, edge_index, W, att_src, att_dst, bias, gamma, beta):
        import jax, jax.numpy as jnp
        import numpy as np
        N, E = (6250, 62500)
        IN_DIM, OUT_DIM, HEADS = (64, 64, 4)
        C = OUT_DIM // HEADS
        NEG_SLOPE = 0.2
        SOFTMAX_EPS = 1e-16
        LN_EPS = 1e-05

        def _gat_forward(x, edge_index, W, att_src, att_dst, bias, gamma, beta):
            src, dst = (edge_index[0], edge_index[1])
            h = (x @ W).reshape(N, HEADS, C)
            a_src = jnp.einsum('nhc,hc->nh', h, att_src)
            a_dst = jnp.einsum('nhc,hc->nh', h, att_dst)
            e = a_src[src] + a_dst[dst]
            e = jnp.where(e >= 0, e, NEG_SLOPE * e)
            m = jax.ops.segment_max(e, dst, num_segments=N)
            m = jnp.where(jnp.isfinite(m), m, 0.0)
            ex = jnp.exp(e - m[dst])
            denom = jax.ops.segment_sum(ex, dst, num_segments=N)
            alpha = ex / (denom[dst] + SOFTMAX_EPS)
            msg = alpha[:, :, None] * h[src]
            out = jax.ops.segment_sum(msg, dst, num_segments=N)
            out = out.reshape(N, HEADS * C) + bias
            mu = out.mean(axis=-1, keepdims=True)
            var = out.var(axis=-1, keepdims=True)
            out = (out - mu) * jax.lax.rsqrt(var + LN_EPS) * gamma + beta
            return out
        return _gat_forward(node_input, edge_index, W, att_src, att_dst, bias, gamma, beta)

    def _L2_gnn_ref(x, edge_index, edge_type, rule_ids, W_r, Wq_w, Wq_bias, Wk_w, Wk_bias, rule_emb, bias, ln_g, ln_b):
        import jax, jax.numpy as jnp
        import numpy as np
        N_NODES = 3125
        N_EDGES = 50000
        IN_DIM = 64
        OUT_DIM = 64
        N_REL = 8
        N_RULES = 32
        N_ACTIVE = 4
        LN_EPS = 1e-05

        def _seg_softmax(scores, seg, num_segments):
            m = jax.ops.segment_max(scores, seg, num_segments=num_segments)
            e = jnp.exp(scores - m[seg])
            d = jax.ops.segment_sum(e, seg, num_segments=num_segments)
            return e / d[seg]
        src, dst = (edge_index[0], edge_index[1])
        num_nodes, in_dim = x.shape
        num_rel, _, out_dim = W_r.shape
        x_src = x[src]
        q = x[dst] @ Wq_w + Wq_bias
        rel_emb = W_r.mean(axis=-1)[edge_type]
        Wk1, Wk2, Wk3 = (Wk_w[:in_dim], Wk_w[in_dim:2 * in_dim], Wk_w[2 * in_dim:])
        key_base = x_src @ Wk1 + rel_emb @ Wk2 + Wk_bias
        h_R = rule_emb[rule_ids]
        key_rule = h_R @ Wk3
        scale = 1.0 / out_dim ** 0.5
        score_base = jnp.einsum('eo,eo->e', q, key_base)
        score_rule = jnp.einsum('eo,ro->er', q, key_rule)
        scores = (score_base[:, None] + score_rule) * scale
        attn = jax.vmap(lambda s: _seg_softmax(s, dst, num_nodes), in_axes=1, out_axes=1)(scores)
        mean_attn = attn.mean(axis=1)
        msg = jnp.zeros((x_src.shape[0], out_dim), dtype=x.dtype)
        for r in range(num_rel):
            msg = jnp.where((edge_type == r)[:, None], x_src @ W_r[r], msg)
        out = jax.ops.segment_sum(msg * mean_attn[:, None], dst, num_segments=num_nodes)
        out = out + bias
        mu = out.mean(axis=-1, keepdims=True)
        var = ((out - mu) ** 2).mean(axis=-1, keepdims=True)
        out = (out - mu) * jax.lax.rsqrt(var + LN_EPS) * ln_g + ln_b
        return jax.nn.relu(out)

    def _L3_gnn_ref(node_embeddings, edge_index, edge_type, task_embedding, Wq, bq, Wk, bk, Wv, bv, ek_tab, ev_tab, es_tab, eg_tab, Wo, bo, ln1_g, ln1_b, W1, b1, W2, b2, ln2_g, ln2_b, Wf, bf):
        import jax, jax.numpy as jnp
        import numpy as np
        N, E, HID, NH, HD, NET = (3125, 50000, 64, 4, 16, 8)

        def _layer_norm(x, g, b, eps=1e-05):
            m = jnp.mean(x, axis=-1, keepdims=True)
            v = jnp.mean((x - m) ** 2, axis=-1, keepdims=True)
            return (x - m) * jax.lax.rsqrt(v + eps) * g + b
        n = node_embeddings.shape[0]
        nh = es_tab.shape[1]
        hd = node_embeddings.shape[1] // nh
        scale = 1.0 / hd ** 0.5
        src, dst = (edge_index[0], edge_index[1])
        q = (node_embeddings @ Wq + bq).reshape(n, nh, hd)
        k = (node_embeddings @ Wk + bk).reshape(n, nh, hd)
        v = (node_embeddings @ Wv + bv).reshape(n, nh, hd)
        e_k = ek_tab[edge_type].reshape(-1, nh, hd)
        e_v = ev_tab[edge_type].reshape(-1, nh, hd)
        logits = jnp.sum(q[dst] * (k[src] + e_k), axis=-1) * scale + es_tab[edge_type]
        logits = logits + jnp.clip(jnp.log(eg_tab[edge_type]), -10.0, 10.0)
        mx = jax.ops.segment_max(logits, dst, num_segments=n)
        mx = jnp.where(jnp.isinf(mx), 0.0, mx)
        ex = jnp.exp(logits - mx[dst])
        sums = jax.ops.segment_sum(ex, dst, num_segments=n)
        attn = ex / jnp.maximum(sums[dst], 1e-12)
        msg = (v[src] + e_v) * attn[..., None]
        agg = jax.ops.segment_sum(msg.reshape(-1, nh * hd), dst, num_segments=n)
        agg = agg @ Wo + bo
        gb = task_embedding @ Wf + bf
        gamma, beta = (gb[:nh * hd], gb[nh * hd:])
        agg = agg * (1.0 + 0.5 * jnp.tanh(gamma))[None, :] + beta[None, :]
        x = _layer_norm(node_embeddings + agg, ln1_g, ln1_b)
        h = jax.nn.gelu(x @ W1 + b1, approximate=False) @ W2 + b2
        return _layer_norm(x + h, ln2_g, ln2_b)
    edge_index = jnp.stack([src, dst])
    x = _layernorm(x + _L0_gnn_ref(x, edge_index, edge_attr_64, L0_gnn_Wl1, L0_gnn_bl1, L0_gnn_Wr1, L0_gnn_br1, L0_gnn_We1, L0_gnn_att1, L0_gnn_bo1, L0_gnn_Wl2, L0_gnn_bl2, L0_gnn_Wr2, L0_gnn_br2, L0_gnn_We2, L0_gnn_att2, L0_gnn_bo2, L0_gnn_Wskip, L0_gnn_bskip), axis=-1)
    x = _layernorm(x + _L1_gnn_ref(x, edge_index, L1_gnn_W, L1_gnn_att_src, L1_gnn_att_dst, L1_gnn_bias, L1_gnn_gamma, L1_gnn_beta), axis=-1)
    x = _layernorm(x + _L2_gnn_ref(x, edge_index, edge_type_8, L2_gnn_rule_ids, L2_gnn_W_r, L2_gnn_Wq_w, L2_gnn_Wq_bias, L2_gnn_Wk_w, L2_gnn_Wk_bias, L2_gnn_rule_emb, L2_gnn_bias, L2_gnn_ln_g, L2_gnn_ln_b), axis=-1)
    x = _layernorm(x + _L3_gnn_ref(x, edge_index, edge_type_8, L3_gnn_task_embedding, L3_gnn_Wq, L3_gnn_bq, L3_gnn_Wk, L3_gnn_bk, L3_gnn_Wv, L3_gnn_bv, L3_gnn_ek_tab, L3_gnn_ev_tab, L3_gnn_es_tab, L3_gnn_eg_tab, L3_gnn_Wo, L3_gnn_bo, L3_gnn_ln1_g, L3_gnn_ln1_b, L3_gnn_W1, L3_gnn_b1, L3_gnn_W2, L3_gnn_b2, L3_gnn_ln2_g, L3_gnn_ln2_b, L3_gnn_Wf, L3_gnn_bf), axis=-1)
    return x

_drawn_inputs = setup_inputs


def setup_inputs(seed=0):
    import zlib

    import numpy as np

    out = dict(_drawn_inputs(seed))
    spreads = {'L1_gnn_bias': (0.0, 0.1),
     'L1_gnn_gamma': (1.0, 0.2),
     'L1_gnn_beta': (0.0, 0.1),
     'L2_gnn_Wq_bias': (0.0, 0.578),
     'L2_gnn_Wk_bias': (0.0, 2.0),
     'L2_gnn_bias': (0.0, 0.1),
     'L2_gnn_ln_g': (1.0, 0.2),
     'L2_gnn_ln_b': (0.0, 0.1),
     'L3_gnn_bq': (0.0, 0.8),
     'L3_gnn_bk': (0.0, 2.0),
     'L3_gnn_bv': (0.0, 0.656),
     'L3_gnn_bo': (0.0, 0.1),
     'L3_gnn_ln1_g': (1.0, 0.2),
     'L3_gnn_ln1_b': (0.0, 0.1),
     'L3_gnn_b1': (0.0, 0.431),
     'L3_gnn_b2': (0.0, 0.1),
     'L3_gnn_ln2_g': (1.0, 0.2),
     'L3_gnn_ln2_b': (0.0, 0.1),
     'L3_gnn_bf': (0.0, 0.1)}
    factors = {'edge_attr_64': 5.641,
     'L0_gnn_Wr1': 8.0,
     'L0_gnn_br1': 8.0,
     'L0_gnn_We1': 6.928,
     'L0_gnn_Wr2': 8.0,
     'L0_gnn_br2': 22.675,
     'L0_gnn_We2': 7.556,
     'L0_gnn_att2': 2.89,
     'L2_gnn_rule_emb': 200.0,
     'L3_gnn_Wq': 8.0,
     'L3_gnn_Wk': 8.0,
     'L3_gnn_ek_tab': 21.789,
     'L3_gnn_ev_tab': 8.0,
     'L3_gnn_es_tab': 55.748,
     'L3_gnn_eg_tab': 200.0}
    for name, (base, spread) in spreads.items():
        noise = np.random.default_rng([zlib.crc32(name.encode()), seed]).standard_normal(out[name].shape)
        drawn = base * np.exp(spread * noise) if base else spread * noise
        out[name] = jnp.asarray(drawn.astype(out[name].dtype))
    for name, factor in factors.items():
        out[name] = (out[name] * factor).astype(out[name].dtype)
    return out
```

```python
from contextlib import ExitStack

import concourse.bass as bass
from concourse import mybir

F32 = mybir.dt.float32
BF16 = mybir.dt.bfloat16
I32 = mybir.dt.int32
U32 = mybir.dt.uint32
ALU = mybir.AluOpType
ACT = mybir.ActivationFunctionType
AX_X = mybir.AxisListType.X

P = 128
N = 6250
E = 200000
D = 64
REL = 8
GROUP = 8
K = -(-N // P)
NPAD = K * P
LASTN = N - (P - 1) * K
BLK = 14
ROWS = 112
TILES = ROWS * BLK
GROUPS = TILES // GROUP
L = BLK * P
WINS = K + 1
BIG = 1.0e38
assert TILES * P >= E and TILES % GROUP == 0 and NPAD > N


def each(eng, n, body):
    body(0, 0)
    body(1, 1)
    turns = (n - 1) // 2
    with eng.Fori(1, turns, 1) as it:
        body(it * 2, 0)
        body(it * 2 + 1, 1)
    for g in range(2 * turns, n):
        body(g, g % 2)


def wait(eng, sem, value):
    if not isinstance(value, int) or value > 0:
        eng.wait_ge(sem, value)


def stage_sem(nc, ctx, name):
    handle = nc.alloc_semaphore(name)

    def clear():
        nc.gpsimd.dma_reset(range(handle.num, handle.num + 1))
        nc.gpsimd.sem_clear(handle)
        nc.release_semaphore(handle)
    ctx.callback(clear)
    return handle


class Chain:

    def __init__(self, eng, sem):
        self.eng, self.sem, self.n = eng, sem, 0

    def __call__(self, ins):
        self.n += 1
        ins.then_inc(self.sem, 1)
        self.eng.wait_ge(self.sem, self.n)


def over(ap, axis, shape):
    return ap.unsqueeze(axis).broadcast_to(shape)


LAYERS = [
    dict(name="a", heads=1, row=64, msg=0, dst=64, rels=1, scale=1.0, eps=1e-16),
    dict(name="b", heads=1, row=64, msg=0, dst=64, rels=1, scale=1.0, eps=1e-16),
    dict(name="c", heads=4, row=68, msg=0, dst=4, rels=1, scale=1.0, eps=1e-16),
    dict(name="d", heads=4, row=128, msg=64, dst=68, rels=REL, scale=0.125, eps=None),
    dict(name="e", heads=4, row=132, msg=64, dst=64, rels=REL, scale=1.0, eps=None),
]

VECS = ["att1", "bo1", "att2", "bo2", "bias1", "gamma1", "beta1", "bias2", "g2", "b2", "bo3",
        "ln1g", "ln1b", "b1lo", "b1hi", "b2v", "ln2g", "ln2b"]


def build(nc, t, out, nlayers=5):
    with ExitStack() as ctx:
        def sb(name, shape, dt=F32, at=ctx):
            return at.enter_context(nc.sbuf_tensor(name, shape, dt))

        def dram(name, shape, dt=F32):
            return nc.dram_tensor(name, shape, dt, kind="Internal").ap()

        m = dict(
            xN=sb("xN", [P, K, D]),
            hN=sb("hN", [P, K, D]),
            skipN=sb("skipN", [P, K, D]),
            perm=sb("perm", [P, K], I32),
            srcI=sb("srcI", [P, TILES], I32),
            typedI=sb("typedI", [P, TILES], I32),
            rel=sb("rel", [P, TILES]),
            win=sb("win", [1, TILES], I32),
            score=sb("score", [P, 4, TILES]),
            ident=sb("ident", [P, P]),
            iota=sb("iota", [P, 2 * P]),
            pid=sb("pid", [P, 2]),
            onesB=sb("onesB", [1, P], BF16),
            vec=sb("vec", [P, len(VECS), D]),
            contP=sb("contP", [ROWS, L], BF16),
            contN=sb("contN", [ROWS, L], BF16),
            first=sb("first", [ROWS, L], BF16),
            last=sb("last", [ROWS, L], BF16),
            edgeC=sb("edgeC", [ROWS, 3]),
            linkF=sb("linkF", [8, ROWS]), linkB=sb("linkB", [8, ROWS]),
            takeF=sb("takeF", [8, ROWS]), takeB=sb("takeB", [8, ROWS]),
        )
        d = dict(
            win=dram("win_d", [TILES], I32),
            perm=dram("perm_d", [P, K], I32),
            rel=dram("rel_d", [ROWS, L], BF16),
            agg=dram("agg_d", [NPAD, D]),
            spill=dram("spill_d", [P, TILES, D]),
        )
        prepare(nc, t, m, d)
        for i, spec in enumerate(LAYERS[:nlayers]):
            table = dram(f"table_{spec['name']}", [NPAD * spec["rels"], spec["row"]])
            with ExitStack() as lay:
                d["dst"] = dram(f"dst_{spec['name']}", [NPAD, spec["dst"]])
                dstW = sb(f"dstW_{spec['name']}", [P, WINS, spec["dst"]], at=lay)
                tables(nc, t, m, d, i, spec, table, dstW)
                scores(nc, t, m, d, i, spec, table, dstW)
            softmax(nc, m, i, spec)
            aggregate(nc, m, d, i, spec)
            finish(nc, t, m, d, i, spec)
        store(nc, m, out)


def prepare(nc, t, m, d):
    with ExitStack() as ctx:
        def sb(name, shape, dt=F32):
            return ctx.enter_context(nc.sbuf_tensor("pr_" + name, shape, dt))

        def sem(name):
            return stage_sem(nc, ctx, "pr_" + name)

        typeI = sb("typeI", [P, TILES], I32)
        dstI = sb("dstI", [P, TILES], I32)
        dstF = sb("dstF", [P, TILES])
        hi = sb("hi", [P, TILES])
        lo = sb("lo", [P, TILES])
        tmpI = sb("tmpI", [P, TILES], I32)
        tmpF = sb("tmpF", [P, TILES])
        rowI = sb("rowI", [ROWS, L + 2], I32)
        rowF = sb("rowF", [ROWS, L + 2])
        cum = sb("cum", [ROWS, L])
        start = sb("start", [ROWS, L])
        ones = sb("ones", [P, L], BF16)
        upper = sb("upper", [P, P])
        allone = sb("allone", [P, P])
        ohHi = [sb(f"ohHi{s}", [P, GROUP, P], BF16) for s in range(2)]
        ohLo = [sb(f"ohLo{s}", [P, GROUP, K], BF16) for s in range(2)]
        zero = sb("zero", [P, P], BF16)
        relS = sb("relS", [ROWS, L])
        relB = sb("relB", [ROWS, L], BF16)
        winF = sb("winF", [ROWS, BLK])
        winQ = sb("winQ", [ROWS, BLK])
        winI = sb("winI", [ROWS, BLK], I32)
        c8 = sb("c8", [ROWS, 3, 8])
        small = sb("small", [P, 8])
        has = sb("has", [P, K])
        before = sb("before", [P, K])
        nid = sb("nid", [P, K])
        permF = sb("permF", [P, K])
        ta = sb("ta", [8, 3, ROWS])
        psH = ctx.enter_context(nc.psum_tensor("pr_psH", [P, 512], F32))
        psT = [ctx.enter_context(nc.psum_tensor(f"pr_psT{s}", [P, 512], F32)) for s in range(2)]
        psS = ctx.enter_context(nc.psum_tensor("pr_psS", [P, 512], F32))
        loaded, made, dch, hot, counted, counts = (sem(n) for n in ("loaded", "made", "dch", "hot", "counted", "counts"))
        sums, offs, turned, back, stored, reload, flagT = (
            sem(n) for n in ("sums", "offs", "turned", "back", "stored", "reload", "flagT"))
        LOADS = 7

        with nc.Block() as block:
            @block.sync
            def _(sp):
                sp.dma_start(dstI[:, :], t["dstT"]).then_inc(loaded, 16)
                sp.dma_start(m["srcI"][:, :], t["srcT"]).then_inc(loaded, 16)
                sp.dma_start(typeI[:, :], t["typeT"]).then_inc(loaded, 16)
                sp.dma_start(rowI[:, :], t["dstS"]).then_inc(loaded, 16)
                sp.dma_start(m["vec"][:, :, :], t["vec"]).then_inc(loaded, 16)
                sp.wait_ge(made, 6)
                sp.dma_start(m["xN"][0:P - 1, :, :], t["x"][0:(P - 1) * K, :].rearrange("(p k) f -> p k f", k=K)).then_inc(loaded, 16)
                sp.dma_start(m["xN"][P - 1:P, 0:LASTN, :], t["x"][(P - 1) * K:N, :].rearrange("(p k) f -> p k f", p=1)).then_inc(loaded, 16)
                sp.wait_ge(back, 1)
                sp.dma_start(d["rel"], relB[:, :]).then_inc(stored, 16)
                sp.dma_start(d["win"].rearrange("(r b) -> r b", b=BLK), winI[:, :]).then_inc(stored, 16)
                sp.wait_ge(stored, 32)
                sp.dma_start(m["win"][:, :], d["win"].rearrange("(a n) -> a n", a=1)).then_inc(reload, 16)
                sp.wait_ge(reload, 16)

            @block.gpsimd
            def _(g):
                g.memset(m["ident"][:, :], 0.0).then_inc(made, 1)
                g.memset(upper[:, :], 1.0).then_inc(made, 1)
                g.memset(allone[:, :], 1.0).then_inc(made, 1)
                g.memset(ones[:, :], 1.0).then_inc(made, 1)
                g.memset(zero[:, :], 0.0).then_inc(made, 1)
                g.memset(m["xN"][:, :, :], 0.0).then_inc(made, 1)
                g.memset(m["onesB"][:, :], 1.0).then_inc(made, 1)
                g.wait_ge(made, 7)
                g.affine_select(out=m["ident"][:, :], in_=m["ident"][:, :], compare_op=ALU.not_equal, fill=1.0,
                                base=0, pattern=[[-1, P]], channel_multiplier=1).then_inc(made, 1)
                g.affine_select(out=upper[:, :], in_=upper[:, :], compare_op=ALU.is_gt, fill=0.0,
                                base=0, pattern=[[1, P]], channel_multiplier=-1).then_inc(made, 1)
                g.iota(m["iota"][:, :], pattern=[[1, 2 * P]], base=0, channel_multiplier=0,
                       allow_small_or_imprecise_dtypes=True).then_inc(made, 1)
                g.iota(m["pid"][:, :], pattern=[[P, 2]], base=0, channel_multiplier=1,
                       allow_small_or_imprecise_dtypes=True).then_inc(made, 1)
                g.iota(nid[:, :], pattern=[[1, K]], base=0, channel_multiplier=K,
                       allow_small_or_imprecise_dtypes=True).then_inc(made, 1)
            MADE = 12

            @block.vector
            def _(v):
                link = Chain(v, dch)

                def floordiv(q, r, x, by, scratchI, scratchF):
                    link(v.tensor_scalar(scratchI, x, 1.0 / by, None, ALU.mult))
                    link(v.tensor_copy(q, scratchI))
                    link(v.scalar_tensor_tensor(r, q, -float(by), x, ALU.mult, ALU.add))
                    link(v.tensor_single_scalar(scratchF, r, 0.0, ALU.is_lt))
                    link(v.tensor_tensor(q, q, scratchF, ALU.subtract))
                    link(v.scalar_tensor_tensor(r, scratchF, float(by), r, ALU.mult, ALU.add))
                    link(v.tensor_single_scalar(scratchF, r, float(by), ALU.is_ge))
                    link(v.tensor_tensor(q, q, scratchF, ALU.add))
                    link(v.scalar_tensor_tensor(r, scratchF, -float(by), r, ALU.mult, ALU.add))

                v.wait_ge(loaded, 16 * LOADS)
                link(v.scalar_tensor_tensor(m["typedI"][:, :], m["srcI"][:, :], float(REL), typeI[:, :], ALU.mult, ALU.add))
                link(v.tensor_copy(dstF[:, :], dstI[:, :]))
                floordiv(hi[:, :], lo[:, :], dstF[:, :], K, tmpI[:, :], tmpF[:, :])
                v.wait_ge(made, MADE)

                def onehots(g, s):
                    wait(v, counted, g - 1)
                    v.tensor_tensor(ohHi[s][:, :, :], over(hi[:, bass.ds(g * GROUP, GROUP)], 2, [P, GROUP, P]),
                                    over(m["iota"][:, 0:P], 1, [P, GROUP, P]), ALU.is_equal).then_inc(hot, 1)
                    v.tensor_tensor(ohLo[s][:, :, :], over(lo[:, bass.ds(g * GROUP, GROUP)], 2, [P, GROUP, K]),
                                    over(m["iota"][:, 0:K], 1, [P, GROUP, K]), ALU.is_equal).then_inc(hot, 1)
                each(v, GROUPS, onehots)

                link(v.tensor_copy(rowF[:, :], rowI[:, :]))
                mid = rowF[:, 1:L + 1]
                link(v.tensor_tensor(m["contP"][:, :], mid, rowF[:, 0:L], ALU.is_equal))
                link(v.tensor_tensor(m["contN"][:, :], mid, rowF[:, 2:L + 2], ALU.is_equal))
                link(v.tensor_scalar(m["first"][:, :], mid, rowF[:, 1:2], None, ALU.is_equal))
                link(v.tensor_scalar(m["last"][:, :], mid, rowF[:, L:L + 1], None, ALU.is_equal))
                link(v.tensor_copy(m["edgeC"][:, 0:1], m["contP"][:, 0:1]))
                link(v.tensor_copy(m["edgeC"][:, 1:2], m["contN"][:, L - 1:L]))
                link(v.tensor_copy(m["edgeC"][:, 2:3], m["first"][:, L - 1:L]))
                v.tensor_copy(c8[:, :, :], over(m["edgeC"][:, :], 2, [ROWS, 3, 8])).then_inc(sums, 1)
                link(v.tensor_scalar(start[:, :], m["contP"][:, :], -1.0, 1.0, ALU.mult, ALU.add))
                link(v.tensor_tensor_scan(cum[:, :], ones[0:ROWS, :], start[:, :], 0.0, ALU.mult, ALU.add))
                v.tensor_copy(small[0:ROWS, 0:1], cum[:, L - 1:L]).then_inc(sums, 1)
                v.wait_ge(flagT, 1)
                link(v.tensor_copy(ta[:, :, :], psT[0][0:8, 0:3 * ROWS].rearrange("a (f r) -> a f r", f=3)))
                R1 = ROWS - 1
                link(v.memset(m["linkF"][:, :], 0.0))
                link(v.memset(m["linkB"][:, :], 0.0))
                link(v.tensor_copy(m["takeF"][:, :], ta[:, 0, :]))
                link(v.tensor_copy(m["takeB"][:, :], ta[:, 1, :]))
                link(v.tensor_tensor(m["linkF"][:, 1:ROWS], ta[:, 0, 1:ROWS], ta[:, 2, 0:R1], ALU.mult))
                link(v.tensor_tensor(m["linkB"][:, 0:R1], ta[:, 1, 0:R1], ta[:, 2, 1:ROWS], ALU.mult))
                v.wait_ge(offs, 1)
                link(v.tensor_scalar(small[0:ROWS, 1:2], psS[0:ROWS, 0:1], -1.0, None, ALU.add))
                link(v.tensor_scalar(cum[:, :], cum[:, :], small[0:ROWS, 1:2], None, ALU.add))
                cum3 = cum[:, :].rearrange("r (b q) -> r b q", q=P)
                link(v.tensor_copy(winQ[:, :], cum3[:, :, 0]))
                floordiv(winF[:, :], tmpF[0:ROWS, 0:BLK], winQ[:, :], P, winI[:, :], tmpF[0:ROWS, 32:32 + BLK])
                link(v.tensor_copy(winI[:, :], winF[:, :]))
                link(v.scalar_tensor_tensor(relS[:, :].rearrange("r (b q) -> r b q", q=P), over(winF[:, :], 2, [ROWS, BLK, P]),
                                            -float(P), cum3, ALU.mult, ALU.add))
                v.tensor_copy(relB[:, :], relS[:, :]).then_inc(back, 1)
                for b in range(BLK):
                    v.wait_ge(turned, b + 1)
                    v.tensor_copy(m["rel"][:, :].rearrange("p (r b) -> p r b", b=BLK)[:, :, b],
                                  psT[b % 2][:, 0:ROWS]).then_inc(back, 1)
                v.wait_ge(counts, 1)
                link(v.tensor_single_scalar(has[:, :], psH[:, 0:K], 0.5, ALU.is_gt))
                link(v.tensor_tensor_scan(before[:, :], ones[:, 0:K], has[:, :], 0.0, ALU.mult, ALU.add))
                v.tensor_copy(small[:, 2:3], before[:, K - 1:K]).then_inc(sums, 1)
                v.wait_ge(sums, 3)
                link(v.tensor_tensor(before[:, :], before[:, :], has[:, :], ALU.subtract))
                v.wait_ge(offs, 3)
                link(v.tensor_copy(small[:, 4:6], psS[:, 4:6]))
                link(v.tensor_scalar(before[:, :], before[:, :], small[:, 4:5], None, ALU.add))
                link(v.scalar_tensor_tensor(permF[:, :], before[:, :], -2.0, nid[:, :], ALU.mult, ALU.add))
                link(v.tensor_scalar(permF[:, :], permF[:, :], small[:, 5:6], None, ALU.add))
                link(v.tensor_scalar(has[:, :], has[:, :], -1.0, 1.0, ALU.mult, ALU.add))
                link(v.tensor_tensor(permF[:, :], permF[:, :], has[:, :], ALU.mult))
                link(v.tensor_tensor(m["perm"][:, :], permF[:, :], before[:, :], ALU.add))

            @block.tensor
            def _(pe):
                pe.wait_ge(made, MADE)
                pe.matmul(psH[:, 0:K], zero[:, :], ones[:, 0:K], start=True, stop=False, skip_group_check=True)

                def count(g, s):
                    pe.wait_ge(hot, g * 2 + 2)
                    for j in range(GROUP):
                        last = pe.matmul(psH[:, 0:K], ohHi[s][:, j, :], ohLo[s][:, j, :], start=False, stop=False,
                                         skip_group_check=True)
                    last.then_inc(counted, 1)
                each(pe, GROUPS, count)
                pe.wait_ge(counted, GROUPS)
                pe.matmul(psH[:, 0:K], zero[:, :], ones[:, 0:K], start=False, stop=True, skip_group_check=True).then_inc(counts, 1)
                pe.wait_ge(sums, 1)
                for f in range(3):
                    last = pe.transpose(psT[0][0:8, f * ROWS:(f + 1) * ROWS], c8[:, f, :], m["ident"][0:ROWS, 0:ROWS])
                last.then_inc(flagT, 1)
                pe.wait_ge(sums, 2)
                pe.matmul(psS[0:ROWS, 0:1], upper[0:ROWS, 0:ROWS], small[0:ROWS, 0:1], start=True, stop=True).then_inc(offs, 1)
                for b in range(BLK):
                    pe.wait_ge(back, max(1, b))
                    pe.transpose(psT[b % 2][:, 0:ROWS], relS[:, b * P:(b + 1) * P], m["ident"][0:ROWS, 0:ROWS]).then_inc(turned, 1)
                pe.wait_ge(sums, 3)
                pe.matmul(psS[:, 4:5], upper[:, :], small[:, 2:3], start=True, stop=True).then_inc(offs, 1)
                pe.matmul(psS[:, 5:6], allone[:, :], small[:, 2:3], start=True, stop=True).then_inc(offs, 1)


def tables(nc, t, m, d, i, spec, table, dstW):
    nm = spec["name"] + "t_"
    rels, row, dc = spec["rels"], spec["row"], spec["dst"]
    xin = m["hN"] if i == 1 else m["xN"]
    with ExitStack() as ctx:
        def sb(name, shape, dt=F32):
            return ctx.enter_context(nc.sbuf_tensor(nm + name, shape, dt))

        def sem(name):
            return stage_sem(nc, ctx, nm + name)

        xT = sb("xT", [D + 1, K * P])
        dstN = sb("dstN", [P, K, dc])
        st = [sb(f"st{s}", [P, rels, row]) for s in range(2)]
        WR = {0: 64, 1: 64, 2: 68, 3: 512, 4: 512}[i]
        wA = sb("wA", [D + 1, WR])
        wD = sb("wD", [D + 1, dc])
        psA = [ctx.enter_context(nc.psum_tensor(f"{nm}psA{s}", [P, 512], F32)) for s in range(2)]
        psB = [ctx.enter_context(nc.psum_tensor(f"{nm}psB{s}", [P, 512], F32)) for s in range(2)]
        psD = [ctx.enter_context(nc.psum_tensor(f"{nm}psD{s}", [P, 512], F32)) for s in range(2)]
        psX = [ctx.enter_context(nc.psum_tensor(f"{nm}psX{s}", [P, 512], F32)) for s in range(2)]
        loaded, turned, copied, ready, prod, tookV, tookA, scat, back, wch, wpe, xch, ruled = (
            sem(n) for n in ("loaded", "turned", "copied", "ready", "prod", "tookV", "tookA", "scat", "back", "wch", "wpe", "xch", "ruled"))
        put = [sem(f"put{s}") for s in range(2)]
        if i == 0:
            wS = sb("wS", [D + 1, D])
        if i == 2:
            wT = sb("wT", [D, D])
            att = sb("att", [D, 8])
        if i >= 3:
            wB = sb("wB", [D + 1, 512])
            w0 = sb("w0", [D, D])
            w1 = sb("w1", [D, D])
            rowA = sb("rowA", [D + 1, 512])
            rowB = sb("rowB", [D + 1, 512])
        if i == 3:
            rm = sb("rm", [D, REL])
            w2 = sb("w2", [D, D])
            ids = sb("ids", [4, 1], I32)
            rule = sb("rule", [4, D])
            ruleT = sb("ruleT", [D, 4])
            keyT = sb("keyT", [D, 4])
            wqT = sb("wqT", [D, D + 1])
        if i == 4:
            wE = sb("wE", [D + 1, REL * 4])
            eg = sb("eg", [D + 1, REL * 4])
            es = sb("es", [D + 1, REL * 4])
        nload = {0: 3, 1: 2, 2: 3, 3: 8, 4: 9}[i]

        with nc.Block() as block:
            @block.sync
            def _(sp):
                def ld(dst, src):
                    sp.dma_start(dst, src).then_inc(loaded, 16)
                if i in (0, 1):
                    ld(wA[:, :], t[f"Wl{i + 1}"])
                    ld(wD[:, :], t[f"Wr{i + 1}"])
                    if i == 0:
                        ld(wS[:, :], t["Wskip"])
                if i == 2:
                    ld(wA[0:D, 0:D], t["gatW"])
                    ld(wT[:, :], t["gatWT"])
                    ld(att[:, :], t["gatAtt"])
                if i == 3:
                    ld(wB[0:D, :], t["Wrel"])
                    ld(w0[:, :], t["Wk"][0:D, :])
                    ld(w1[:, :], t["Wk"][D:2 * D, :])
                    ld(w2[:, :], t["Wk"][2 * D:3 * D, :])
                    ld(wD[:, 0:D], t["Wq2"])
                    ld(wqT[:, :], t["Wq2T"])
                    ld(rowA[D:D + 1, :].rearrange("a (r f) -> a r f", f=D), over(t["bk2"].rearrange("(a f) -> a f", a=1), 1, [1, REL, D]))
                    ld(ids[:, :], t["ruleids"].rearrange("(r a) -> r a", a=1))
                if i == 4:
                    ld(w0[:, :], t["Wk3"])
                    ld(w1[:, :], t["Wv3"])
                    ld(wD[:, :], t["Wq3"])
                    ld(rowA[D:D + 1, :].rearrange("a (r f) -> a r f", f=D), over(t["bk3"].rearrange("(a f) -> a f", a=1), 1, [1, REL, D]))
                    ld(rowB[D:D + 1, :].rearrange("a (r f) -> a r f", f=D), over(t["bv3"].rearrange("(a f) -> a f", a=1), 1, [1, REL, D]))
                    ld(wA[D:D + 1, :], t["ek"].rearrange("(a r) f -> a (r f)", a=1))
                    ld(wB[D:D + 1, :], t["ev"].rearrange("(a r) f -> a (r f)", a=1))
                    ld(es[D:D + 1, :], t["es"].rearrange("(a r) f -> a (r f)", a=1))
                    ld(eg[D:D + 1, :], t["eg"].rearrange("(a r) f -> a (r f)", a=1))
                rows = table.rearrange("(p k r) c -> p k (r c)", k=K, r=rels)

                def put_rows(k, s):
                    sp.wait_ge(tookV, k + 1)
                    sp.wait_ge(tookA, k + 1)
                    sp.dma_start(rows[:, bass.ds(k, 1), :], st[s][:, :, :].rearrange("p (a r) c -> p a (r c)", a=1)).then_inc(put[s], 16)
                each(sp, K, put_rows)
                sp.wait_ge(put[0], 16 * ((K + 1) // 2))
                sp.wait_ge(put[1], 16 * (K // 2))
                sp.wait_ge(scat, 16 * K)
                sp.dma_start(dstW[:, 0:K, :], d["dst"].rearrange("(w p) c -> p w c", p=P)).then_inc(back, 16)
                sp.wait_ge(back, 16)

            @block.gpsimd
            def _(g):
                g.memset(dstW[:, K:WINS, :], 0.0).then_inc(xch, 1)
                if i == 3:
                    g.wait_ge(loaded, 16 * nload)
                    g.indirect_dma_start(rule[:, :], None, t["ruleemb"],
                                         bass.IndirectOffsetOnAxis(ap=ids[:, :].bitcast(U32), axis=0)).then_inc(ruled, 16)
                g.wait_ge(tookA, K)
                for k in range(K):
                    g.indirect_dma_start(d["dst"], bass.IndirectOffsetOnAxis(ap=m["perm"][:, k:k + 1].bitcast(U32), axis=0),
                                         dstN[:, k, :], None).then_inc(scat, 16)

            @block.vector
            def _(v):
                link = Chain(v, wch)
                v.memset(xT[D:D + 1, :], 1.0).then_inc(xch, 1)
                for c in range(-(-K // 4)):
                    n = min(4, K - 4 * c)
                    v.wait_ge(turned, c + 1)
                    v.tensor_copy(xT[0:D, c * 4 * P:(c * 4 + n) * P], psX[c % 2][0:D, 0:n * P]).then_inc(copied, 1)
                v.wait_ge(loaded, 16 * nload)
                if i == 2:
                    link(v.memset(wA[D:D + 1, :], 0.0))
                    link(v.memset(wD[D:D + 1, :], 0.0))
                    v.wait_ge(wpe, 1)
                    link(v.tensor_copy(wA[0:D, D:D + 4], psA[0][0:D, 0:4]))
                    link(v.tensor_copy(wD[0:D, :], psA[0][0:D, 4:8]))
                if i >= 3:
                    link(v.tensor_copy(wA[0:D, :].rearrange("p (r f) -> p r f", f=D), over(w0[:, :], 1, [D, REL, D])))
                if i == 3:
                    link(v.memset(wB[D:D + 1, :], 0.0))
                    link(v.tensor_reduce(rm[:, :], wB[0:D, :].rearrange("p (r f) -> p r f", f=D), AX_X, ALU.add))
                    v.tensor_scalar(rm[:, :], rm[:, :], 1.0 / D, None, ALU.mult).then_inc(ready, 1)
                    v.wait_ge(wpe, 1)
                    link(v.tensor_copy(ruleT[:, :], psB[0][0:D, 0:4]))
                    link(v.tensor_tensor(wA[D:D + 1, :], psA[0][D:D + 1, :], rowA[D:D + 1, :], ALU.add))
                    v.sem_inc(ready, 1)
                    v.wait_ge(wpe, 2)
                    link(v.tensor_copy(keyT[:, :], psB[0][0:D, 8:12]))
                    v.sem_inc(ready, 1)
                    v.wait_ge(wpe, 3)
                    link(v.tensor_copy(wD[:, D:D + 4], psB[0][0:D + 1, 16:20]))
                if i == 4:
                    link(v.tensor_copy(wB[0:D, :].rearrange("p (r f) -> p r f", f=D), over(w1[:, :], 1, [D, REL, D])))
                    link(v.tensor_tensor(wA[D:D + 1, :], wA[D:D + 1, :], rowA[D:D + 1, :], ALU.add))
                    link(v.tensor_tensor(wB[D:D + 1, :], wB[D:D + 1, :], rowB[D:D + 1, :], ALU.add))
                    link(v.memset(wE[0:D, :], 0.0))
                    v.wait_ge(wpe, 1)
                    link(v.tensor_scalar(eg[D:D + 1, :], eg[D:D + 1, :], 10.0, -10.0, ALU.min, ALU.max))
                    link(v.tensor_tensor(wE[D:D + 1, :], eg[D:D + 1, :], es[D:D + 1, :], ALU.add))
                v.sem_inc(ready, 1)

                def take(k, s):
                    v.wait_ge(prod, k + 1)
                    wait(v, put[s], (k - s) * 8)
                    if i <= 2:
                        v.tensor_copy(st[s][:, 0, :], psA[s][:, 0:row]).then_inc(tookV, 1)
                    else:
                        v.tensor_copy(st[s][:, :, 0:D], psA[s][:, :].rearrange("p (r f) -> p r f", f=D)).then_inc(tookV, 1)
                each(v, K, take)

            @block.scalar
            def _(a):
                if i == 4:
                    a.wait_ge(loaded, 16 * nload)
                    a.activation(eg[D:D + 1, :], eg[D:D + 1, :], ACT.Ln).then_inc(wpe, 1)

                def take(k, s):
                    a.wait_ge(prod, k + 1)
                    if i >= 3:
                        wait(a, put[s], (k - s) * 8)
                        a.activation(st[s][:, :, D:2 * D], psB[s][:, :].rearrange("p (r f) -> p r f", f=D), ACT.Copy)
                    if i == 4:
                        a.activation(st[s][:, :, 2 * D:2 * D + 4], psD[s][:, 128:160].rearrange("p (r h) -> p r h", h=4), ACT.Copy)
                    if i == 0:
                        a.activation(m["skipN"][:, bass.ds(k, 1), :], psD[s][:, 128:192].rearrange("p (a f) -> p a f", a=1), ACT.Copy)
                    a.activation(dstN[:, bass.ds(k, 1), :], psD[s][:, 0:dc].rearrange("p (a f) -> p a f", a=1), ACT.Copy).then_inc(tookA, 1)
                each(a, K, take)

            @block.tensor
            def _(pe):
                for c in range(-(-K // 4)):
                    if c >= 2:
                        pe.wait_ge(copied, c - 1)
                    for k in range(4 * c, min(4 * c + 4, K)):
                        last = pe.transpose(psX[c % 2][0:D, (k % 4) * P:(k % 4 + 1) * P], xin[:, k, :], m["ident"][:, :])
                    last.then_inc(turned, 1)
                if i == 2:
                    pe.wait_ge(loaded, 16 * nload)
                    pe.matmul(psA[0][0:D, 0:8], wT[:, :], att[:, :], start=True, stop=True).then_inc(wpe, 1)
                if i == 3:
                    pe.wait_ge(ready, 1)
                    pe.wait_ge(ruled, 16)
                    for r in range(REL):
                        pe.matmul(psA[0][D:D + 1, r * D:(r + 1) * D], rm[:, r:r + 1], w1[:, :], start=True, stop=True)
                    pe.transpose(psB[0][0:D, 0:4], rule[:, :], m["ident"][0:4, 0:4]).then_inc(wpe, 1)
                    pe.wait_ge(ready, 2)
                    pe.matmul(psB[0][0:D, 8:12], w2[:, :], ruleT[:, :], start=True, stop=True).then_inc(wpe, 1)
                    pe.wait_ge(ready, 3)
                    pe.matmul(psB[0][0:D + 1, 16:20], wqT[:, :], keyT[:, :], start=True, stop=True).then_inc(wpe, 1)
                pe.wait_ge(xch, 2)
                pe.wait_ge(copied, -(-K // 4))
                pe.wait_ge(ready, 4 if i == 3 else 1)

                def products(k, s):
                    wait(pe, tookV, k - 1)
                    wait(pe, tookA, k - 1)
                    x = xT[:, k * P:(k + 1) * P]
                    pe.matmul(psA[s][:, 0:WR], x, wA[:, :], start=True, stop=True)
                    if i >= 3:
                        pe.matmul(psB[s][:, :], x, wB[:, :], start=True, stop=True)
                    if i == 4:
                        pe.matmul(psD[s][:, 128:160], x, wE[:, :], start=True, stop=True)
                    if i == 0:
                        pe.matmul(psD[s][:, 128:192], x, wS[:, :], start=True, stop=True)
                    pe.matmul(psD[s][:, 0:dc], x, wD[:, :], start=True, stop=True).then_inc(prod, 1)
                for k in range(K):
                    products(k, k % 2)


def scores(nc, t, m, d, i, spec, table, dstW):
    nm = spec["name"] + "s_"
    row, msg, dc, H = spec["row"], spec["msg"], spec["dst"], spec["heads"]
    idx = m["srcI"] if i <= 2 else m["typedI"]
    relrow = d["rel"].rearrange("(a r) e -> a (r e)", a=1)
    with ExitStack() as ctx:
        def sb(name, shape, dt=F32):
            return ctx.enter_context(nc.sbuf_tensor(nm + name, shape, dt))

        def sem(name):
            return stage_sem(nc, ctx, nm + name)

        GE = GROUP * P
        gat = [sb(f"gat{s}", [P, GROUP, row]) for s in range(2)]
        idxS = [sb(f"idx{s}", [P, GROUP], I32) for s in range(2)]
        rank = [sb(f"rank{s}", [1, GE], BF16) for s in range(2)]
        hot = [sb(f"hot{s}", [P, 2, GE]) for s in range(2)]
        mid = [sb(f"mid{s}", [P, GROUP, D]) for s in range(2)]
        act = [sb(f"act{s}", [P, GROUP, D]) for s in range(2)]
        red = [sb(f"red{s}", [P, GROUP, 4]) for s in range(2)]
        if i <= 1:
            ea = [sb(f"ea{s}", [D, GE]) for s in range(2)]
            we = sb("we", [D, D])
        DW = 64 if i <= 2 else 128
        psR = [ctx.enter_context(nc.psum_tensor(f"{nm}psR{s}", [P, GE], F32)) for s in range(2)]
        psM = [ctx.enter_context(nc.psum_tensor(f"{nm}psM{s}", [P, GROUP * DW], F32)) for s in range(2)]
        staged, spread, hots, made, used, ch, pch, wl = (
            sem(n) for n in ("staged", "spread", "hots", "made", "used", "ch", "pch", "wl"))
        got = [sem(f"got{s}") for s in range(2)]
        spilt = [sem(f"spilt{s}") for s in range(2)]
        fed = [sem(f"fed{s}") for s in range(2)]
        FEED = 32 if i <= 1 else 16

        with nc.Block() as block:
            @block.sync
            def _(sp):
                if i <= 1:
                    sp.dma_start(we[:, :], t[f"We{i + 1}"]).then_inc(wl, 16)

                def feed(g, s):
                    wait(sp, made, g - 1)
                    sp.dma_start(rank[s][:, :], relrow[:, bass.ds(g * GE, GE)]).then_inc(fed[s], 16)
                    if i <= 1:
                        sp.dma_start(ea[s][:, :], t["eaT"][:, bass.ds(g * GE, GE)]).then_inc(fed[s], 16)
                each(sp, GROUPS, feed)

            @block.scalar
            def _(a):
                def stage(g, s):
                    wait(a, got[s], (g - s) * 64)
                    a.activation(idxS[s][:, :], idx[:, bass.ds(g * GROUP, GROUP)], ACT.Copy).then_inc(staged, 1)

                def step(g, s):
                    if not isinstance(g, int) or g < GROUPS - 1:
                        stage(g + 1, 1 - s)
                    a.wait_ge(got[s], (g - s) * 64 + 128)
                    a.dma_start(d["spill"][:, bass.ds(g * GROUP, GROUP), :], gat[s][:, :, msg:msg + D]).then_inc(spilt[s], 16)
                stage(0, 0)
                each(a, GROUPS, step)
                for s in range(2):
                    a.wait_ge(spilt[s], 16 * (GROUPS // 2))

            @block.gpsimd
            def _(g_):
                def gather(g, s):
                    g_.wait_ge(staged, g + 1)
                    wait(g_, used, g - 1)
                    wait(g_, spilt[s], (g - s) * 8)
                    g_.sem_inc(pch, 1)
                    for j in range(GROUP):
                        g_.indirect_dma_start(gat[s][:, j, :], None, table,
                                              bass.IndirectOffsetOnAxis(ap=idxS[s][:, j:j + 1].bitcast(U32), axis=0)).then_inc(got[s], 16)
                each(g_, GROUPS, gather)

            @block.vector
            def _(v):
                def onehot(g, s):
                    v.wait_ge(spread, g + 1)
                    wait(v, made, g - 1)
                    for a in range(2):
                        v.tensor_scalar(hot[s][:, a, :], psR[s][:, :], m["pid"][:, a:a + 1], None, ALU.is_equal).then_inc(hots, 1)

                LINKS = {0: 3, 1: 3, 2: 1, 3: 2, 4: 2}[i]

                def score(g, s):
                    k = [0]

                    def link(ins):
                        k[0] += 1
                        ins.then_inc(ch, 1)
                        v.wait_ge(ch, g * LINKS + k[0])

                    v.wait_ge(made, g + 1)
                    v.wait_ge(got[s], (g - s) * 64 + 128)
                    dst3 = psM[s][:, :].rearrange("p (j c) -> p j c", c=DW)
                    outp = m["score"][:, :, bass.ds(g * GROUP, GROUP)].rearrange("p h j -> p j h")
                    if i <= 1:
                        link(v.tensor_tensor(mid[s][:, :, :], dst3, gat[s][:, :, :], ALU.add))
                        link(v.scalar_tensor_tensor(act[s][:, :, :], mid[s][:, :, :], 0.2, mid[s][:, :, :], ALU.mult, ALU.max))
                        link(v.tensor_tensor(mid[s][:, :, :], act[s][:, :, :], over(m["vec"][:, VECS.index(f"att{i + 1}"), :], 1, [P, GROUP, D]), ALU.mult))
                        v.tensor_reduce(m["score"][:, 0, bass.ds(g * GROUP, GROUP)], mid[s][:, :, :], AX_X, ALU.add).then_inc(used, 1)
                    elif i == 2:
                        link(v.tensor_tensor(red[s][:, :, :], dst3[:, :, 0:4], gat[s][:, :, D:D + 4], ALU.add))
                        v.scalar_tensor_tensor(outp, red[s][:, :, :], 0.2, red[s][:, :, :], ALU.mult, ALU.max).then_inc(used, 1)
                    elif i == 3:
                        link(v.tensor_tensor(mid[s][:, :, :], dst3[:, :, 0:D], gat[s][:, :, 0:D], ALU.mult))
                        link(v.tensor_reduce(red[s][:, :, 0:1], mid[s][:, :, :], AX_X, ALU.add))
                        v.tensor_tensor(outp, dst3[:, :, D:D + 4], red[s][:, :, 0:1].broadcast_to([P, GROUP, 4]), ALU.add).then_inc(used, 1)
                    else:
                        link(v.tensor_tensor(mid[s][:, :, :], dst3[:, :, 0:D], gat[s][:, :, 0:D], ALU.mult))
                        link(v.tensor_reduce(red[s][:, :, :], mid[s][:, :, :].rearrange("p j (h c) -> p j h c", h=4), AX_X, ALU.add))
                        v.scalar_tensor_tensor(outp, red[s][:, :, :], 0.25, gat[s][:, :, 2 * D:2 * D + 4], ALU.mult, ALU.add).then_inc(used, 1)

                def step(g, s):
                    if not isinstance(g, int) or g < GROUPS - 1:
                        onehot(g + 1, 1 - s)
                    score(g, s)
                onehot(0, 0)
                each(v, GROUPS, step)

            @block.tensor
            def _(pe):
                def spread_ranks(g, s):
                    pe.wait_ge(fed[s], (g - s) * (FEED // 2) + FEED)
                    wait(pe, hots, g * 2 - 2)
                    for c in range(2):
                        last = pe.matmul(psR[s][:, c * 512:(c + 1) * 512], m["onesB"][:, :], rank[s][:, c * 512:(c + 1) * 512],
                                         start=True, stop=True)
                    last.then_inc(spread, 1)

                def step(g, s):
                    if not isinstance(g, int) or g < GROUPS - 1:
                        spread_ranks(g + 1, 1 - s)
                    pe.wait_ge(hots, g * 2 + 2)
                    wait(pe, used, g - 1)
                    for j in range(GROUP):
                        w = pe.value_load(m["win"][0:1, bass.ds(g * GROUP + j, 1)], min_val=0, max_val=WINS - 2)
                        o = psM[s][:, j * DW:j * DW + dc]
                        for a in range(2):
                            last = pe.matmul(o, hot[s][:, a, j * P:(j + 1) * P],
                                             dstW[:, bass.ds(w + a, 1), :], start=(a == 0), stop=(a == 1 and i > 1))
                        if i <= 1:
                            last = pe.matmul(o, ea[s][:, j * P:(j + 1) * P], we[:, :], start=False, stop=True)
                    last.then_inc(made, 1)
                if i <= 1:
                    pe.wait_ge(wl, 16)
                spread_ranks(0, 0)
                each(pe, GROUPS, step)


def softmax(nc, m, i, spec):
    nm = spec["name"] + "x_"
    H = spec["heads"]
    with ExitStack() as ctx:
        def sb(name, shape, dt=F32):
            return ctx.enter_context(nc.sbuf_tensor(nm + name, shape, dt))

        def sem(name):
            return stage_sem(nc, ctx, nm + name)

        X = sb("X", [ROWS, H, L])
        A = sb("A", [ROWS, H, L])
        B = sb("B", [ROWS, H, L])
        pen = sb("pen", [ROWS, L], BF16)
        pen2 = sb("pen2", [ROWS, L], BF16)
        ends = sb("ends", [ROWS, 8])
        endT = sb("endT", [8, ROWS + 2])
        carr = sb("carr", [8, 2, ROWS])
        lnk = sb("lnk", [8, ROWS])
        tk = sb("tk", [8, ROWS])
        carry = sb("carry", [ROWS, 16])
        psT = [ctx.enter_context(nc.psum_tensor(f"{nm}psT{s}", [P, 512], F32)) for s in range(2)]
        psE = ctx.enter_context(nc.psum_tensor(f"{nm}psE", [P, 512], F32))
        turned, copied, ch, want, gave, sub, exped, wback, turned2, ptr = (
            sem(n) for n in ("turned", "copied", "ch", "want", "gave", "sub", "exped", "wback", "turned2", "ptr"))
        scoreT = m["score"][:, :, :].rearrange("p h (r b) -> p h r b", b=BLK)
        NT = 7 * H // 2 if (7 * H) % 2 == 0 else None
        steps = [(h, b) for h in range(H) for b in range(BLK)]
        HOUT = 1 if i == 3 else H
        osteps = [(h, b) for h in range(HOUT) for b in range(BLK)]

        with nc.Block() as block:
            @block.scalar
            def _(a):
                for n, (h, b) in enumerate(steps):
                    a.wait_ge(turned, n + 1)
                    a.activation(X[:, h, b * P:(b + 1) * P], psT[n % 2][0:ROWS, 0:P], ACT.Copy, scale=spec["scale"]).then_inc(copied, 1)
                for h in range(H):
                    a.wait_ge(sub, h + 1)
                    a.activation(X[:, h, :], X[:, h, :], ACT.Exp).then_inc(exped, 1)
                for n, (h, b) in enumerate(osteps):
                    a.wait_ge(turned2, n + 1)
                    a.activation(scoreT[:, h, :, b], psT[n % 2][:, 0:ROWS], ACT.Copy).then_inc(wback, 1)

            @block.tensor
            def _(pe):
                for n, (h, b) in enumerate(steps):
                    if n >= 2:
                        pe.wait_ge(copied, n - 1)
                    pe.transpose(psT[n % 2][0:ROWS, 0:P], scoreT[:, h, :, b], m["ident"][:, :]).then_inc(turned, 1)
                for q in range(2):
                    pe.wait_ge(want, 2 * q + 1)
                    pe.transpose(psE[0:8, 0:ROWS], ends[:, :], m["ident"][0:ROWS, 0:ROWS]).then_inc(gave, 1)
                    pe.wait_ge(want, 2 * q + 2)
                    for x in range(2):
                        last = pe.transpose(psE[0:ROWS, 128 + 8 * x:136 + 8 * x], carr[:, x, :], m["ident"][0:8, 0:8])
                    last.then_inc(gave, 1)
                pe.wait_ge(copied, len(steps))
                pe.wait_ge(ptr, 1)
                for n, (h, b) in enumerate(osteps):
                    if n >= 2:
                        pe.wait_ge(wback, n - 1)
                    pe.transpose(psT[n % 2][:, 0:ROWS], X[:, h, b * P:(b + 1) * P], m["ident"][0:ROWS, 0:ROWS]).then_inc(turned2, 1)

            @block.vector
            def _(v):
                link = Chain(v, ch)

                def segments(q, biggest):
                    if biggest:
                        link(v.tensor_scalar(pen[:, :], m["contP"][:, :], BIG, -BIG, ALU.mult, ALU.add))
                        link(v.tensor_scalar(pen2[:, :], m["contN"][:, :], BIG, -BIG, ALU.mult, ALU.add))
                    for h in range(H):
                        if biggest:
                            link(v.tensor_tensor_scan(A[:, h, :], pen[:, :], X[:, h, :], -BIG, ALU.add, ALU.max))
                            link(v.tensor_tensor_scan(B[:, h, ::-1], pen2[:, ::-1], A[:, h, ::-1], -BIG, ALU.add, ALU.max))
                        else:
                            link(v.tensor_tensor_scan(A[:, h, :], m["contP"][:, :], X[:, h, :], 0.0, ALU.mult, ALU.add))
                            link(v.tensor_tensor(A[:, h, :], A[:, h, :], pen2[:, :], ALU.mult))
                            link(v.tensor_tensor_scan(B[:, h, ::-1], m["contN"][:, ::-1], A[:, h, ::-1], 0.0, ALU.mult, ALU.add))
                    link(v.memset(ends[:, :], 0.0))
                    link(v.tensor_copy(ends[:, 0:H], B[:, :, 0]))
                    v.tensor_copy(ends[:, 4:4 + H], B[:, :, L - 1]).then_inc(want, 1)
                    v.wait_ge(gave, 2 * q + 1)
                    link(v.memset(endT[:, :], 0.0))
                    link(v.tensor_copy(endT[:, 1:ROWS + 1], psE[0:8, 0:ROWS]))
                    for x, (link_, take, lo, rev) in enumerate(((m["linkF"], m["takeF"], 0, 1), (m["linkB"], m["takeB"], 2, -1))):
                        nb = endT[:, lo:lo + ROWS]
                        if biggest:
                            link(v.tensor_scalar(lnk[:, :], link_[:, :], BIG, -BIG, ALU.mult, ALU.add))
                            link(v.tensor_scalar(tk[:, :], take[:, :], BIG, -BIG, ALU.mult, ALU.add))
                            link(v.tensor_tensor(tk[:, :], tk[:, :], nb, ALU.add))
                            link(v.tensor_tensor_scan(carr[:, x, ::rev], lnk[:, ::rev], tk[:, ::rev], -BIG, ALU.add, ALU.max))
                        else:
                            link(v.tensor_tensor(tk[:, :], take[:, :], nb, ALU.mult))
                            link(v.tensor_tensor_scan(carr[:, x, ::rev], link_[:, ::rev], tk[:, ::rev], 0.0, ALU.mult, ALU.add))
                    v.sem_inc(want, 1)
                    v.wait_ge(gave, 2 * q + 2)
                    link(v.tensor_copy(carry[:, :], psE[0:ROWS, 128:144]))
                    for mask, at in ((m["first"], 4), (m["last"], 8)):
                        if biggest:
                            link(v.tensor_scalar(pen[:, :], mask[:, :], BIG, -BIG, ALU.mult, ALU.add))
                        for h in range(H):
                            c = carry[:, at + h:at + h + 1]
                            if biggest:
                                link(v.scalar_tensor_tensor(B[:, h, :], pen[:, :], c, B[:, h, :], ALU.add, ALU.max))
                            else:
                                link(v.scalar_tensor_tensor(B[:, h, :], mask[:, :], c, B[:, h, :], ALU.mult, ALU.add))

                v.wait_ge(copied, len(steps))
                segments(0, True)
                for h in range(H):
                    v.tensor_tensor(X[:, h, :], X[:, h, :], B[:, h, :], ALU.subtract).then_inc(sub, 1)
                link(v.tensor_scalar(pen2[:, :], m["contN"][:, :], -1.0, 1.0, ALU.mult, ALU.add))
                link(v.memset(pen2[:, L - 1:L], 1.0))
                v.wait_ge(exped, H)
                segments(1, False)
                for h in range(H):
                    if i == 4:
                        link(v.tensor_scalar_max(B[:, h, :], B[:, h, :], 1e-12))
                    elif spec["eps"]:
                        link(v.tensor_scalar_add(B[:, h, :], B[:, h, :], spec["eps"]))
                    link(v.reciprocal(A[:, h, :], B[:, h, :]))
                    link(v.tensor_tensor(X[:, h, :], X[:, h, :], A[:, h, :], ALU.mult))
                if i == 3:
                    link(v.tensor_tensor(A[:, 0, :], X[:, 0, :], X[:, 1, :], ALU.add))
                    link(v.tensor_tensor(A[:, 1, :], X[:, 2, :], X[:, 3, :], ALU.add))
                    link(v.tensor_tensor(A[:, 0, :], A[:, 0, :], A[:, 1, :], ALU.add))
                    link(v.tensor_scalar(X[:, 0, :], A[:, 0, :], 0.25, None, ALU.mult))
                v.sem_inc(ptr, 1)


def aggregate(nc, m, d, i, spec):
    nm = spec["name"] + "g_"
    H = 1 if i == 3 else spec["heads"]
    with ExitStack() as ctx:
        def sb(name, shape, dt=F32):
            return ctx.enter_context(nc.sbuf_tensor(nm + name, shape, dt))

        def sem(name):
            return stage_sem(nc, ctx, nm + name)

        msgs = [sb(f"msg{s}", [P, GROUP, D]) for s in range(2)]
        wtd = [sb(f"wtd{s}", [P, GROUP, D]) for s in range(2)]
        hot = [sb(f"hot{s}", [P, GROUP, 2 * P]) for s in range(2)]
        zero = sb("zero", [P, 512])
        outS = sb("outS", [P, K, D])
        BANKS = -(-WINS * D // 512)
        psG = ctx.enter_context(nc.psum_tensor(nm + "psG", [P, BANKS * 512], F32))
        zeroed, ready, summed, done, copied, stored = (sem(n) for n in ("zeroed", "ready", "summed", "done", "copied", "stored"))
        fed = [sem(f"fed{s}") for s in range(2)]

        with nc.Block() as block:
            @block.sync
            def _(sp):
                def feed(g, s):
                    wait(sp, ready, g * 2 - 2)
                    sp.dma_start(msgs[s][:, :, :], d["spill"][:, bass.ds(g * GROUP, GROUP), :]).then_inc(fed[s], 16)
                each(sp, GROUPS, feed)
                sp.wait_ge(copied, 1)
                sp.dma_start(d["agg"].rearrange("(w p) f -> p w f", p=P), outS[:, :, :]).then_inc(stored, 16)
                sp.wait_ge(stored, 16)

            @block.vector
            def _(v):
                v.memset(zero[:, :], 0.0).then_inc(zeroed, 1)

                def step(g, s):
                    wait(v, summed, g - 1)
                    v.tensor_tensor(hot[s][:, :, :], over(m["rel"][:, bass.ds(g * GROUP, GROUP)], 2, [P, GROUP, 2 * P]),
                                    over(m["iota"][:, :], 1, [P, GROUP, 2 * P]), ALU.is_equal).then_inc(ready, 1)
                    v.wait_ge(fed[s], (g - s) * 8 + 16)
                    if H == 1:
                        v.tensor_tensor(wtd[s][:, :, :], msgs[s][:, :, :],
                                        over(m["score"][:, 0, bass.ds(g * GROUP, GROUP)], 2, [P, GROUP, D]), ALU.mult).then_inc(ready, 1)
                    else:
                        al = m["score"][:, :, bass.ds(g * GROUP, GROUP)].rearrange("p h j -> p j h")
                        v.tensor_tensor(wtd[s][:, :, :].rearrange("p j (h c) -> p j h c", h=4),
                                        msgs[s][:, :, :].rearrange("p j (h c) -> p j h c", h=4),
                                        over(al, 3, [P, GROUP, 4, D // 4]), ALU.mult).then_inc(ready, 1)
                each(v, GROUPS, step)
                v.wait_ge(done, 1)
                v.tensor_copy(outS[:, :, :].rearrange("p w f -> p (w f)"), psG[:, 0:K * D]).then_inc(copied, 1)

            @block.tensor
            def _(pe):
                pe.wait_ge(zeroed, 1)
                for b in range(BANKS):
                    pe.matmul(psG[:, b * 512:(b + 1) * 512], zero[:, 0:P], zero[:, :], start=True, stop=False, skip_group_check=True)

                def step(g, s):
                    pe.wait_ge(ready, g * 2 + 2)
                    for j in range(GROUP):
                        w = pe.value_load(m["win"][0:1, bass.ds(g * GROUP + j, 1)], min_val=0, max_val=WINS - 2)
                        for a in range(2):
                            last = pe.matmul(psG[:, bass.ds((w + a) * D, D)], hot[s][:, j, a * P:(a + 1) * P], wtd[s][:, j, :],
                                             start=False, stop=False, skip_group_check=True)
                    last.then_inc(summed, 1)
                each(pe, GROUPS, step)
                for b in range(BANKS):
                    last = pe.matmul(psG[:, b * 512:(b + 1) * 512], zero[:, 0:P], zero[:, :], start=False, stop=True, skip_group_check=True)
                last.then_inc(done, 1)


def finish(nc, t, m, d, i, spec):
    nm = spec["name"] + "f_"
    with ExitStack() as ctx:
        def sb(name, shape, dt=F32):
            return ctx.enter_context(nc.sbuf_tensor(nm + name, shape, dt))

        def sem(name):
            return stage_sem(nc, ctx, nm + name)

        Y = sb("Y", [P, K, D])
        Q = sb("Q", [P, K, D])
        mean = sb("mean", [P, K])
        var = sb("var", [P, K])
        rstd = sb("rstd", [P, K])
        eps = sb("eps", [P, 1])
        got, ch, asked, rooted, loaded, turned, copied, proj, took, act = (
            sem(n) for n in ("got", "ch", "asked", "rooted", "loaded", "turned", "copied", "proj", "took", "act"))
        if i == 4:
            xT = sb("xT", [P, K * P])
            x1 = sb("x1", [P, K, D])
            hid = [sb(f"hid{s}", [P, P]) for s in range(2)]
            wO = sb("wO", [D, D])
            w1 = sb("w1", [D + 1, 2 * D])
            w2 = sb("w2", [2 * D, D])
            wf = sb("wf", [D + 1, 2 * D])
            task = sb("task", [D + 1, P])
            gb = sb("gb", [P, 2 * D])
            psX = [ctx.enter_context(nc.psum_tensor(f"{nm}psX{s}", [P, 512], F32)) for s in range(2)]
            psP = [ctx.enter_context(nc.psum_tensor(f"{nm}psP{s}", [P, 512], F32)) for s in range(2)]
            psF = ctx.enter_context(nc.psum_tensor(f"{nm}psF", [P, 512], F32))
        NC = -(-K // 4)

        with nc.Block() as block:
            @block.gpsimd
            def _(g):
                for k in range(K):
                    g.indirect_dma_start(Y[:, k, :], None, d["agg"],
                                         bass.IndirectOffsetOnAxis(ap=m["perm"][:, k:k + 1].bitcast(U32), axis=0)).then_inc(got, 16)

            if i == 4:
                @block.sync
                def _(sp):
                    sp.dma_start(wO[:, :], t["Wo3"]).then_inc(loaded, 16)
                    sp.dma_start(w1[:, :], t["W1"]).then_inc(loaded, 16)
                    sp.dma_start(w2[:, :], t["W2"]).then_inc(loaded, 16)
                    sp.dma_start(wf[:, :], t["Wf"]).then_inc(loaded, 16)
                    sp.dma_start(task[:, :], t["task"]).then_inc(loaded, 16)

                @block.tensor
                def _(pe):
                    pe.wait_ge(loaded, 80)
                    pe.matmul(psF[:, 0:2 * D], task[:, :], wf[:, :], start=True, stop=True).then_inc(proj, 1)

                    def turn(src, base):
                        for c in range(NC):
                            if base + c >= 2:
                                pe.wait_ge(copied, base + c - 1)
                            for k in range(4 * c, min(4 * c + 4, K)):
                                last = pe.transpose(psX[(base + c) % 2][0:D, (k % 4) * P:(k % 4 + 1) * P], src[:, k, :], m["ident"][:, :])
                            last.then_inc(turned, 1)
                    pe.wait_ge(got, 16 * K)
                    turn(Y, 0)
                    pe.wait_ge(copied, NC)

                    def outp(k, s):
                        wait(pe, took, k - 1)
                        pe.matmul(psP[s][:, 0:D], xT[0:D, k * P:(k + 1) * P], wO[:, :], start=True, stop=True).then_inc(proj, 1)
                    for k in range(K):
                        outp(k, k % 2)
                    pe.wait_ge(asked, 2)
                    turn(x1, NC)
                    pe.wait_ge(copied, 2 * NC)

                    def ffn(k, s):
                        wait(pe, act, k - 1)
                        pe.matmul(psX[s][:, 0:P], w1[:, :], xT[0:D + 1, bass.ds(k * P, P)], start=True, stop=True).then_inc(turned, 1)
                        pe.wait_ge(act, k + 1)
                        pe.wait_ge(took, k + K - 1)
                        pe.matmul(psP[s][:, 0:D], hid[s][:, :], w2[:, :], start=True, stop=True).then_inc(proj, 1)
                    each(pe, K, ffn)

            @block.scalar
            def _(a):
                n = {0: 1, 1: 2, 2: 2, 3: 2, 4: 1}[i]
                if i == 4:
                    a.wait_ge(proj, 1)
                    a.activation(gb[:, 0:D], psF[:, 0:D], ACT.Tanh).then_inc(rooted, 1)
                    a.wait_ge(asked, 1)
                    a.activation(rstd[:, :], var[:, :], ACT.Sqrt, bias=eps[:, 0:1]).then_inc(rooted, 1)

                    def gelu(k, s):
                        a.wait_ge(turned, k + 2 * NC + 1)
                        wait(a, proj, k + K)
                        a.activation(hid[s][:, :], psX[s][:, 0:P], ACT.Gelu).then_inc(act, 1)
                    each(a, K, gelu)
                    for q in range(2):
                        a.wait_ge(asked, 3 + q)
                        a.activation(rstd[:, :], var[:, :], ACT.Sqrt, bias=eps[:, 0:1]).then_inc(rooted, 1)
                else:
                    for q in range(n):
                        a.wait_ge(asked, q + 1)
                        a.activation(rstd[:, :], var[:, :], ACT.Sqrt, bias=eps[:, 0:1]).then_inc(rooted, 1)

            @block.vector
            def _(v):
                link = Chain(v, ch)
                roots = [1 if i == 4 else 0]
                full = [P, K, D]

                def vec(name):
                    return over(m["vec"][:, VECS.index(name), :], 1, full)

                def norm(dst, src):
                    link(v.tensor_reduce(mean[:, :], src[:, :, :], AX_X, ALU.add))
                    link(v.tensor_scalar(mean[:, :], mean[:, :], -1.0 / D, None, ALU.mult))
                    link(v.tensor_tensor(dst[:, :, :], src[:, :, :], over(mean[:, :], 2, full), ALU.add))
                    link(v.tensor_tensor(Q[:, :, :], dst[:, :, :], dst[:, :, :], ALU.mult))
                    link(v.tensor_reduce(var[:, :], Q[:, :, :], AX_X, ALU.add))
                    v.tensor_scalar(var[:, :], var[:, :], 1.0 / D, None, ALU.mult).then_inc(asked, 1)
                    roots[0] += 1
                    v.wait_ge(rooted, roots[0])
                    link(v.reciprocal(mean[:, :], rstd[:, :]))
                    link(v.tensor_tensor(dst[:, :, :], dst[:, :, :], over(mean[:, :], 2, full), ALU.mult))

                xN = m["xN"]
                link(v.memset(eps[:, :], 1e-5))
                v.wait_ge(got, 16 * K)
                if i == 0:
                    link(v.tensor_tensor(Y[:, :, :], Y[:, :, :], vec("bo1"), ALU.add))
                    link(v.tensor_scalar_max(Y[:, :, :], Y[:, :, :], 0.0))
                    norm(m["hN"], Y)
                if i == 1:
                    link(v.tensor_tensor(Y[:, :, :], Y[:, :, :], vec("bo2"), ALU.add))
                    link(v.tensor_tensor(Y[:, :, :], Y[:, :, :], m["skipN"][:, :, :], ALU.add))
                    link(v.tensor_scalar_max(Y[:, :, :], Y[:, :, :], 0.0))
                    norm(Y, Y)
                if i == 2:
                    link(v.tensor_tensor(Y[:, :, :], Y[:, :, :], vec("bias1"), ALU.add))
                    norm(Y, Y)
                    link(v.tensor_tensor(Y[:, :, :], Y[:, :, :], vec("gamma1"), ALU.mult))
                    link(v.tensor_tensor(Y[:, :, :], Y[:, :, :], vec("beta1"), ALU.add))
                if i == 3:
                    link(v.tensor_tensor(Y[:, :, :], Y[:, :, :], vec("bias2"), ALU.add))
                    norm(Y, Y)
                    link(v.tensor_tensor(Y[:, :, :], Y[:, :, :], vec("g2"), ALU.mult))
                    link(v.tensor_tensor(Y[:, :, :], Y[:, :, :], vec("b2"), ALU.add))
                    link(v.tensor_scalar_max(Y[:, :, :], Y[:, :, :], 0.0))
                if i in (1, 2, 3):
                    link(v.tensor_tensor(Y[:, :, :], Y[:, :, :], xN[:, :, :], ALU.add))
                    norm(xN, Y)
                if i == 4:
                    def pull(base):
                        for c in range(NC):
                            n = min(4, K - 4 * c)
                            v.wait_ge(turned, base + c + 1)
                            v.tensor_copy(xT[0:D, c * 4 * P:(c * 4 + n) * P], psX[(base + c) % 2][0:D, 0:n * P]).then_inc(copied, 1)
                    link(v.memset(xT[D:D + 1, :], 1.0))
                    pull(0)
                    v.wait_ge(rooted, 1)
                    link(v.tensor_scalar(gb[:, 0:D], gb[:, 0:D], 0.5, 1.0, ALU.mult, ALU.add))
                    link(v.tensor_copy(gb[:, D:2 * D], psF[:, D:2 * D]))

                    def take_out(k, s):
                        v.wait_ge(proj, k + 2)
                        v.tensor_copy(Q[:, bass.ds(k, 1), :], psP[s][:, 0:D].rearrange("p (a f) -> p a f", a=1)).then_inc(took, 1)
                    each(v, K, take_out)
                    v.wait_ge(took, K)
                    link(v.tensor_tensor(Y[:, :, :], Q[:, :, :], vec("bo3"), ALU.add))
                    link(v.tensor_tensor(Y[:, :, :], Y[:, :, :], over(gb[:, 0:D], 1, full), ALU.mult))
                    link(v.tensor_tensor(Y[:, :, :], Y[:, :, :], over(gb[:, D:2 * D], 1, full), ALU.add))
                    link(v.tensor_tensor(Y[:, :, :], Y[:, :, :], xN[:, :, :], ALU.add))
                    norm(x1, Y)
                    link(v.tensor_tensor(x1[:, :, :], x1[:, :, :], vec("ln1g"), ALU.mult))
                    link(v.tensor_tensor(x1[:, :, :], x1[:, :, :], vec("ln1b"), ALU.add))
                    v.sem_inc(asked, 1)
                    pull(NC)

                    def take_ffn(k, s):
                        v.wait_ge(proj, k + K + 2)
                        v.tensor_copy(Q[:, bass.ds(k, 1), :], psP[s][:, 0:D].rearrange("p (a f) -> p a f", a=1)).then_inc(took, 1)
                    each(v, K, take_ffn)
                    v.wait_ge(took, 2 * K)
                    link(v.tensor_tensor(Y[:, :, :], Q[:, :, :], vec("b2v"), ALU.add))
                    link(v.tensor_tensor(Y[:, :, :], Y[:, :, :], x1[:, :, :], ALU.add))
                    norm(Y, Y)
                    link(v.tensor_tensor(Y[:, :, :], Y[:, :, :], vec("ln2g"), ALU.mult))
                    link(v.tensor_tensor(Y[:, :, :], Y[:, :, :], vec("ln2b"), ALU.add))
                    link(v.tensor_tensor(Y[:, :, :], Y[:, :, :], xN[:, :, :], ALU.add))
                    norm(xN, Y)


def store(nc, m, out):
    with ExitStack() as ctx:
        kept = stage_sem(nc, ctx, "kept")
        with nc.Block() as block:
            @block.sync
            def _(sp):
                sp.dma_start(out[0:(P - 1) * K, :].rearrange("(p k) f -> p k f", k=K), m["xN"][0:P - 1, :, :]).then_inc(kept, 16)
                sp.dma_start(out[(P - 1) * K:N, :].rearrange("(p k) f -> p k f", p=1), m["xN"][P - 1:P, 0:LASTN, :]).then_inc(kept, 16)
                sp.wait_ge(kept, 32)


def kernel(**inp):
    import numpy as np
    import concourse.bacc as bacc
    from concourse.bass_utils import run_bass_kernel_spmd as run

    a = {k: np.asarray(v) for k, v in inp.items()}
    pad = TILES * P - E

    def tiled(v, fill):
        return np.concatenate([v, np.full((pad,), fill, v.dtype)]).reshape(TILES, P).T

    def aug(w, b):
        return np.concatenate([w, b[None, :]], axis=0)

    end = np.full((1,), -1, a["dst"].dtype)
    line = np.concatenate([end, a["dst"], np.full((pad,), N, a["dst"].dtype), end])
    arrays = {
        "x": a["x"], "srcT": tiled(a["src"], 0), "typeT": tiled(a["edge_type_8"], 0), "dstT": tiled(a["dst"], N),
        "dstS": np.stack([line[r * L:(r + 1) * L + 2] for r in range(ROWS)]),
        "eaT": np.concatenate([a["edge_attr_64"], np.zeros((pad, D), np.float32)]).T,
        "Wl1": aug(a["L0_gnn_Wl1"].T, a["L0_gnn_bl1"]), "Wr1": aug(a["L0_gnn_Wr1"].T, a["L0_gnn_br1"]),
        "Wl2": aug(a["L0_gnn_Wl2"].T, a["L0_gnn_bl2"]), "Wr2": aug(a["L0_gnn_Wr2"].T, a["L0_gnn_br2"]),
        "Wskip": aug(a["L0_gnn_Wskip"].T, a["L0_gnn_bskip"]),
        "We1": a["L0_gnn_We1"].T, "We2": a["L0_gnn_We2"].T,
        "gatW": a["L1_gnn_W"], "gatWT": a["L1_gnn_W"].T,
        "Wrel": a["L2_gnn_W_r"].transpose(1, 0, 2).reshape(D, REL * D), "Wk": a["L2_gnn_Wk_w"],
        "Wq2": aug(a["L2_gnn_Wq_w"], a["L2_gnn_Wq_bias"]), "Wq2T": aug(a["L2_gnn_Wq_w"], a["L2_gnn_Wq_bias"]).T,
        "bk2": a["L2_gnn_Wk_bias"], "ruleids": a["L2_gnn_rule_ids"], "ruleemb": a["L2_gnn_rule_emb"],
        "Wk3": a["L3_gnn_Wk"], "Wv3": a["L3_gnn_Wv"], "Wq3": aug(a["L3_gnn_Wq"], a["L3_gnn_bq"]),
        "bk3": a["L3_gnn_bk"], "bv3": a["L3_gnn_bv"], "ek": a["L3_gnn_ek_tab"], "ev": a["L3_gnn_ev_tab"],
        "es": a["L3_gnn_es_tab"], "eg": a["L3_gnn_eg_tab"], "Wo3": a["L3_gnn_Wo"],
        "W1": aug(a["L3_gnn_W1"], a["L3_gnn_b1"]), "W2": a["L3_gnn_W2"], "Wf": aug(a["L3_gnn_Wf"], a["L3_gnn_bf"]),
        "task": np.broadcast_to(np.concatenate([a["L3_gnn_task_embedding"], np.ones((1,), np.float32)])[:, None], (D + 1, P)),
    }
    att = np.zeros((D, 8), np.float32)
    for h in range(4):
        att[h * 16:(h + 1) * 16, h] = a["L1_gnn_att_src"][h]
        att[h * 16:(h + 1) * 16, 4 + h] = a["L1_gnn_att_dst"][h]
    arrays["gatAtt"] = att
    vec = {"att1": "L0_gnn_att1", "bo1": "L0_gnn_bo1", "att2": "L0_gnn_att2", "bo2": "L0_gnn_bo2", "bias1": "L1_gnn_bias",
           "gamma1": "L1_gnn_gamma", "beta1": "L1_gnn_beta", "bias2": "L2_gnn_bias", "g2": "L2_gnn_ln_g", "b2": "L2_gnn_ln_b",
           "bo3": "L3_gnn_bo", "ln1g": "L3_gnn_ln1_g", "ln1b": "L3_gnn_ln1_b", "b1lo": "L3_gnn_b2", "b1hi": "L3_gnn_b2",
           "b2v": "L3_gnn_b2", "ln2g": "L3_gnn_ln2_g", "ln2b": "L3_gnn_ln2_b"}
    arrays["vec"] = np.broadcast_to(np.stack([a[vec[n]] for n in VECS])[None], (P, len(VECS), D))

    nc = bacc.Bacc("TRN2", target_bir_lowering=False, num_devices=1)
    fed, t = {}, {}
    for name, v in arrays.items():
        v = np.ascontiguousarray(v)
        fed[f"in_{name}"] = v
        t[name] = nc.dram_tensor(f"in_{name}", v.shape, mybir.dt.from_np(v.dtype), kind="ExternalInput").ap()
    out = nc.dram_tensor("out_0", (N, D), F32, kind="ExternalOutput").ap()
    build(nc, t, out)
    r = run(nc, [fed], core_ids=[0])
    return r.results[0]["out_0"]
```

```python
from contextlib import ExitStack

import concourse.bass as bass
from concourse import mybir

F32 = mybir.dt.float32
BF16 = mybir.dt.bfloat16
I32 = mybir.dt.int32
U32 = mybir.dt.uint32
ALU = mybir.AluOpType
ACT = mybir.ActivationFunctionType
AX_X = mybir.AxisListType.X

P = 128
N = 6250
E = 200000
D = 64
REL = 8
GROUP = 8
K = -(-N // P)
NPAD = K * P
LASTN = N - (P - 1) * K
BLK = 14
ROWS = 112
TILES = ROWS * BLK
GROUPS = TILES // GROUP
L = BLK * P
RING = 4
GOT = 16 * GROUP
WINS = K + 1
BIG = 1.0e38
assert TILES * P >= E and TILES % GROUP == 0 and NPAD > N


def each(eng, n, body, depth=2):
    for g in range(depth):
        body(g, g)
    turns = (n - 1) // depth
    with eng.Fori(1, turns, 1) as it:
        for s in range(depth):
            body(it * depth + s, s)
    for g in range(depth * turns, n):
        body(g, g % depth)


def wait(eng, sem, value):
    if not isinstance(value, int) or value > 0:
        eng.wait_ge(sem, value)


def stage_sem(nc, ctx, name):
    handle = nc.alloc_semaphore(name)

    def clear():
        nc.gpsimd.dma_reset(range(handle.num, handle.num + 1))
        nc.gpsimd.sem_clear(handle)
        nc.release_semaphore(handle)
    ctx.callback(clear)
    return handle


class Chain:

    def __init__(self, eng, sem):
        self.eng, self.sem, self.n = eng, sem, 0

    def __call__(self, ins):
        self.n += 1
        ins.then_inc(self.sem, 1)
        self.eng.wait_ge(self.sem, self.n)


def load_windows(nc, m, g):
    _, values = nc.values_load_multi_w_load_instructions(
        m["win"][0:1, bass.ds(g * GROUP, GROUP)], engines=(mybir.EngineType.PE,), min_val=0, max_val=WINS - 2,
        skip_runtime_bounds_check_because="windows are computed on the chip from ranks below NPAD")
    return values


def over(ap, axis, shape):
    return ap.unsqueeze(axis).broadcast_to(shape)


LAYERS = [
    dict(name="a", heads=1, row=64, msg=0, dst=64, rels=1, scale=1.0, eps=1e-16),
    dict(name="b", heads=1, row=64, msg=0, dst=64, rels=1, scale=1.0, eps=1e-16),
    dict(name="c", heads=4, row=68, msg=0, dst=4, rels=1, scale=1.0, eps=1e-16),
    dict(name="d", heads=4, row=128, msg=64, dst=68, rels=REL, scale=0.125, eps=None),
    dict(name="e", heads=4, row=132, msg=64, dst=64, rels=REL, scale=1.0, eps=None),
]

VECS = ["att1", "bo1", "att2", "bo2", "bias1", "gamma1", "beta1", "bias2", "g2", "b2", "bo3",
        "ln1g", "ln1b", "b2v", "ln2g", "ln2b"]


def build(nc, t, out, nlayers=5):
    with ExitStack() as ctx:
        def sb(name, shape, dt=F32, at=ctx):
            return at.enter_context(nc.sbuf_tensor(name, shape, dt))

        def dram(name, shape, dt=F32):
            return nc.dram_tensor(name, shape, dt, kind="Internal").ap()

        m = dict(
            xN=sb("xN", [P, K, D]),
            hN=sb("hN", [P, K, D]),
            skipN=sb("skipN", [P, K, D]),
            perm=sb("perm", [P, K], I32),
            srcI=sb("srcI", [P, TILES], I32),
            typedI=sb("typedI", [P, TILES], I32),
            rel=sb("rel", [P, TILES]),
            win=sb("win", [1, TILES], I32),
            score=sb("score", [P, 4, TILES]),
            ident=sb("ident", [P, P]),
            iota=sb("iota", [P, 2 * P]),
            iotaB=sb("iotaB", [P, 2 * P], BF16),
            pid=sb("pid", [P, 2]),
            onesB=sb("onesB", [1, P], BF16),
            vec=sb("vec", [P, len(VECS), D]),
            contP=sb("contP", [ROWS, L], BF16),
            contN=sb("contN", [ROWS, L], BF16),
            first=sb("first", [ROWS, L], BF16),
            last=sb("last", [ROWS, L], BF16),
            edgeC=sb("edgeC", [ROWS, 3]),
            linkF=sb("linkF", [8, ROWS]), linkB=sb("linkB", [8, ROWS]),
            takeF=sb("takeF", [8, ROWS]), takeB=sb("takeB", [8, ROWS]),
        )
        d = dict(
            win=dram("win_d", [TILES], I32),
            rel=dram("rel_d", [ROWS, L], BF16),
            agg=dram("agg_d", [NPAD, D]),
            spill=dram("spill_d", [P, TILES, D]),
        )
        prepare(nc, t, m, d)
        for i, spec in enumerate(LAYERS[:nlayers]):
            table = dram(f"table_{spec['name']}", [NPAD * spec["rels"], spec["row"]])
            with ExitStack() as lay:
                d["dst"] = dram(f"dst_{spec['name']}", [NPAD, spec["dst"]])
                dstW = sb(f"dstW_{spec['name']}", [P, 3, WINS, spec["dst"]], BF16, at=lay)
                tables(nc, t, m, d, i, spec, table, dstW)
                scores(nc, t, m, d, i, spec, table, dstW)
            softmax(nc, m, i, spec)
            aggregate(nc, m, d, i, spec)
            finish(nc, t, m, d, i, spec)
        store(nc, m, out)


def prepare(nc, t, m, d):
    with ExitStack() as ctx:
        def sb(name, shape, dt=F32):
            return ctx.enter_context(nc.sbuf_tensor("pr_" + name, shape, dt))

        def sem(name):
            return stage_sem(nc, ctx, "pr_" + name)

        typeI = sb("typeI", [P, TILES], I32)
        dstI = sb("dstI", [P, TILES], I32)
        hi = sb("hi", [P, TILES])
        lo = sb("lo", [P, TILES])
        hiB = sb("hiB", [P, TILES], BF16)
        loB = sb("loB", [P, TILES], BF16)
        tmpI = sb("tmpI", [P, TILES], I32)
        tmpF = sb("tmpF", [P, TILES])
        rowI = sb("rowI", [ROWS, L + 2], I32)
        rowF = sb("rowF", [ROWS, L + 2])
        cum = sb("cum", [ROWS, L])
        start = sb("start", [ROWS, L])
        ones = sb("ones", [P, L], BF16)
        upper = sb("upper", [P, P])
        allone = sb("allone", [P, P])
        ohHi = [sb(f"ohHi{s}", [P, GROUP, P], BF16) for s in range(2)]
        ohLo = [sb(f"ohLo{s}", [P, GROUP, K], BF16) for s in range(2)]
        zero = sb("zero", [P, P], BF16)
        relS = sb("relS", [ROWS, L])
        relB = sb("relB", [ROWS, L], BF16)
        winF = sb("winF", [ROWS, BLK])
        winQ = sb("winQ", [ROWS, BLK])
        winI = sb("winI", [ROWS, BLK], I32)
        c8 = sb("c8", [ROWS, 3, 8])
        small = sb("small", [P, 8])
        has = sb("has", [P, K])
        before = sb("before", [P, K])
        nid = sb("nid", [P, K])
        permF = sb("permF", [P, K])
        ta = sb("ta", [8, 3, ROWS])
        psH = ctx.enter_context(nc.psum_tensor("pr_psH", [P, 512], F32))
        psT = [ctx.enter_context(nc.psum_tensor(f"pr_psT{s}", [P, 512], F32)) for s in range(2)]
        psS = ctx.enter_context(nc.psum_tensor("pr_psS", [P, 512], F32))
        loaded, made, dch, hot, counted, counts = (sem(n) for n in ("loaded", "made", "dch", "hot", "counted", "counts"))
        sums, offs, turned, back, stored, reload, flagT = (
            sem(n) for n in ("sums", "offs", "turned", "back", "stored", "reload", "flagT"))
        LOADS = 7

        MADE = 13

        with nc.Block() as block:
            @block.sync
            def _(sp):
                sp.dma_start(dstI[:, :], t["dstT"]).then_inc(loaded, 16)
                sp.dma_start(m["srcI"][:, :], t["srcT"]).then_inc(loaded, 16)
                sp.dma_start(typeI[:, :], t["typeT"]).then_inc(loaded, 16)
                sp.dma_start(rowI[:, :], t["dstS"]).then_inc(loaded, 16)
                sp.dma_start(m["vec"][:, :, :], t["vec"]).then_inc(loaded, 16)
                sp.wait_ge(made, 6)
                sp.dma_start(m["xN"][0:P - 1, :, :], t["x"][0:(P - 1) * K, :].rearrange("(p k) f -> p k f", k=K)).then_inc(loaded, 16)
                sp.dma_start(m["xN"][P - 1:P, 0:LASTN, :], t["x"][(P - 1) * K:N, :].rearrange("(p k) f -> p k f", p=1)).then_inc(loaded, 16)
                sp.wait_ge(back, 1)
                sp.dma_start(d["rel"], relB[:, :]).then_inc(stored, 16)
                sp.dma_start(d["win"].rearrange("(r b) -> r b", b=BLK), winI[:, :]).then_inc(stored, 16)
                sp.wait_ge(stored, 32)
                sp.dma_start(m["win"][:, :], d["win"].rearrange("(a n) -> a n", a=1)).then_inc(reload, 16)
                sp.wait_ge(reload, 16)

            @block.gpsimd
            def _(g):
                g.memset(m["ident"][:, :], 0.0).then_inc(made, 1)
                g.memset(upper[:, :], 1.0).then_inc(made, 1)
                g.memset(allone[:, :], 1.0).then_inc(made, 1)
                g.memset(ones[:, :], 1.0).then_inc(made, 1)
                g.memset(zero[:, :], 0.0).then_inc(made, 1)
                g.memset(m["xN"][:, :, :], 0.0).then_inc(made, 1)
                g.memset(m["onesB"][:, :], 1.0).then_inc(made, 1)
                g.wait_ge(made, 7)
                g.affine_select(out=m["ident"][:, :], in_=m["ident"][:, :], compare_op=ALU.not_equal, fill=1.0,
                                base=0, pattern=[[-1, P]], channel_multiplier=1).then_inc(made, 1)
                g.affine_select(out=upper[:, :], in_=upper[:, :], compare_op=ALU.is_gt, fill=0.0,
                                base=0, pattern=[[1, P]], channel_multiplier=-1).then_inc(made, 1)
                g.iota(m["iota"][:, :], pattern=[[1, 2 * P]], base=0, channel_multiplier=0,
                       allow_small_or_imprecise_dtypes=True).then_inc(made, 1)
                g.iota(m["iotaB"][:, :], pattern=[[1, 2 * P]], base=0, channel_multiplier=0,
                       allow_small_or_imprecise_dtypes=True).then_inc(made, 1)
                g.iota(m["pid"][:, :], pattern=[[P, 2]], base=0, channel_multiplier=1,
                       allow_small_or_imprecise_dtypes=True).then_inc(made, 1)
                g.iota(nid[:, :], pattern=[[1, K]], base=0, channel_multiplier=K,
                       allow_small_or_imprecise_dtypes=True).then_inc(made, 1)

            @block.vector
            def _(v):
                link = Chain(v, dch)

                def floordiv(q, r, x, by, scratchI, scratchF):
                    link(v.tensor_scalar(scratchI, x, 1.0 / by, None, ALU.mult))
                    link(v.tensor_copy(q, scratchI))
                    link(v.scalar_tensor_tensor(r, q, -float(by), x, ALU.mult, ALU.add))
                    link(v.tensor_single_scalar(scratchF, r, 0.0, ALU.is_lt))
                    link(v.tensor_tensor(q, q, scratchF, ALU.subtract))
                    link(v.scalar_tensor_tensor(r, scratchF, float(by), r, ALU.mult, ALU.add))
                    link(v.tensor_single_scalar(scratchF, r, float(by), ALU.is_ge))
                    link(v.tensor_tensor(q, q, scratchF, ALU.add))
                    link(v.scalar_tensor_tensor(r, scratchF, -float(by), r, ALU.mult, ALU.add))

                v.wait_ge(loaded, 16 * LOADS)
                link(v.scalar_tensor_tensor(m["typedI"][:, :], m["srcI"][:, :], float(REL), typeI[:, :], ALU.mult, ALU.add))
                link(v.tensor_copy(lo[:, :], dstI[:, :]))
                floordiv(hi[:, :], lo[:, :], lo[:, :], K, tmpI[:, :], tmpF[:, :])
                v.wait_ge(made, MADE)

                link(v.tensor_copy(hiB[:, :], hi[:, :]))
                link(v.tensor_copy(loB[:, :], lo[:, :]))
                def onehots(g, s):
                    wait(v, counted, g - 1)
                    v.tensor_tensor(ohHi[s][:, :, :], over(hiB[:, bass.ds(g * GROUP, GROUP)], 2, [P, GROUP, P]),
                                    over(m["iotaB"][:, 0:P], 1, [P, GROUP, P]), ALU.is_equal).then_inc(hot, 1)
                    v.tensor_tensor(ohLo[s][:, :, :], over(loB[:, bass.ds(g * GROUP, GROUP)], 2, [P, GROUP, K]),
                                    over(m["iotaB"][:, 0:K], 1, [P, GROUP, K]), ALU.is_equal).then_inc(hot, 1)
                each(v, GROUPS, onehots)

                link(v.tensor_copy(rowF[:, :], rowI[:, :]))
                mid = rowF[:, 1:L + 1]
                link(v.tensor_tensor(m["contP"][:, :], mid, rowF[:, 0:L], ALU.is_equal))
                link(v.tensor_tensor(m["contN"][:, :], mid, rowF[:, 2:L + 2], ALU.is_equal))
                link(v.tensor_scalar(m["first"][:, :], mid, rowF[:, 1:2], None, ALU.is_equal))
                link(v.tensor_scalar(m["last"][:, :], mid, rowF[:, L:L + 1], None, ALU.is_equal))
                link(v.tensor_copy(m["edgeC"][:, 0:1], m["contP"][:, 0:1]))
                link(v.tensor_copy(m["edgeC"][:, 1:2], m["contN"][:, L - 1:L]))
                link(v.tensor_copy(m["edgeC"][:, 2:3], m["first"][:, L - 1:L]))
                v.tensor_copy(c8[:, :, :], over(m["edgeC"][:, :], 2, [ROWS, 3, 8])).then_inc(sums, 1)
                link(v.tensor_scalar(start[:, :], m["contP"][:, :], -1.0, 1.0, ALU.mult, ALU.add))
                link(v.tensor_tensor_scan(cum[:, :], ones[0:ROWS, :], start[:, :], 0.0, ALU.mult, ALU.add))
                v.tensor_copy(small[0:ROWS, 0:1], cum[:, L - 1:L]).then_inc(sums, 1)
                v.wait_ge(flagT, 1)
                link(v.tensor_copy(ta[:, :, :], psT[0][0:8, 0:3 * ROWS].rearrange("a (f r) -> a f r", f=3)))
                R1 = ROWS - 1
                link(v.memset(m["linkF"][:, :], 0.0))
                link(v.memset(m["linkB"][:, :], 0.0))
                link(v.tensor_copy(m["takeF"][:, :], ta[:, 0, :]))
                link(v.tensor_copy(m["takeB"][:, :], ta[:, 1, :]))
                link(v.tensor_tensor(m["linkF"][:, 1:ROWS], ta[:, 0, 1:ROWS], ta[:, 2, 0:R1], ALU.mult))
                link(v.tensor_tensor(m["linkB"][:, 0:R1], ta[:, 1, 0:R1], ta[:, 2, 1:ROWS], ALU.mult))
                v.wait_ge(offs, 1)
                link(v.tensor_scalar(small[0:ROWS, 1:2], psS[0:ROWS, 0:1], -1.0, None, ALU.add))
                link(v.tensor_scalar(cum[:, :], cum[:, :], small[0:ROWS, 1:2], None, ALU.add))
                cum3 = cum[:, :].rearrange("r (b q) -> r b q", q=P)
                link(v.tensor_copy(winQ[:, :], cum3[:, :, 0]))
                floordiv(winF[:, :], tmpF[0:ROWS, 0:BLK], winQ[:, :], P, winI[:, :], tmpF[0:ROWS, 32:32 + BLK])
                link(v.tensor_copy(winI[:, :], winF[:, :]))
                link(v.scalar_tensor_tensor(relS[:, :].rearrange("r (b q) -> r b q", q=P), over(winF[:, :], 2, [ROWS, BLK, P]),
                                            -float(P), cum3, ALU.mult, ALU.add))
                v.tensor_copy(relB[:, :], relS[:, :]).then_inc(back, 1)
                for b in range(BLK):
                    v.wait_ge(turned, b + 1)
                    v.tensor_copy(m["rel"][:, :].rearrange("p (r b) -> p r b", b=BLK)[:, :, b],
                                  psT[b % 2][:, 0:ROWS]).then_inc(back, 1)
                v.wait_ge(counts, 1)
                link(v.tensor_single_scalar(has[:, :], psH[:, 0:K], 0.5, ALU.is_gt))
                link(v.tensor_tensor_scan(before[:, :], ones[:, 0:K], has[:, :], 0.0, ALU.mult, ALU.add))
                v.tensor_copy(small[:, 2:3], before[:, K - 1:K]).then_inc(sums, 1)
                v.wait_ge(sums, 3)
                link(v.tensor_tensor(before[:, :], before[:, :], has[:, :], ALU.subtract))
                v.wait_ge(offs, 3)
                link(v.tensor_copy(small[:, 4:6], psS[:, 4:6]))
                link(v.tensor_scalar(before[:, :], before[:, :], small[:, 4:5], None, ALU.add))
                link(v.scalar_tensor_tensor(permF[:, :], before[:, :], -2.0, nid[:, :], ALU.mult, ALU.add))
                link(v.tensor_scalar(permF[:, :], permF[:, :], small[:, 5:6], None, ALU.add))
                link(v.tensor_scalar(has[:, :], has[:, :], -1.0, 1.0, ALU.mult, ALU.add))
                link(v.tensor_tensor(permF[:, :], permF[:, :], has[:, :], ALU.mult))
                link(v.tensor_tensor(m["perm"][:, :], permF[:, :], before[:, :], ALU.add))

            @block.tensor
            def _(pe):
                pe.wait_ge(made, MADE)
                pe.matmul(psH[:, 0:K], zero[:, :], ones[:, 0:K], start=True, stop=False, skip_group_check=True)

                def count(g, s):
                    pe.wait_ge(hot, g * 2 + 2)
                    for j in range(GROUP):
                        last = pe.matmul(psH[:, 0:K], ohHi[s][:, j, :], ohLo[s][:, j, :], start=False, stop=False,
                                         skip_group_check=True)
                    last.then_inc(counted, 1)
                each(pe, GROUPS, count)
                pe.wait_ge(counted, GROUPS)
                pe.matmul(psH[:, 0:K], zero[:, :], ones[:, 0:K], start=False, stop=True, skip_group_check=True).then_inc(counts, 1)
                pe.wait_ge(sums, 1)
                for f in range(3):
                    last = pe.transpose(psT[0][0:8, f * ROWS:(f + 1) * ROWS], c8[:, f, :], m["ident"][0:ROWS, 0:ROWS])
                last.then_inc(flagT, 1)
                pe.wait_ge(sums, 2)
                pe.matmul(psS[0:ROWS, 0:1], upper[0:ROWS, 0:ROWS], small[0:ROWS, 0:1], start=True, stop=True).then_inc(offs, 1)
                for b in range(BLK):
                    pe.wait_ge(back, max(1, b))
                    pe.transpose(psT[b % 2][:, 0:ROWS], relS[:, b * P:(b + 1) * P], m["ident"][0:ROWS, 0:ROWS]).then_inc(turned, 1)
                pe.wait_ge(sums, 3)
                pe.matmul(psS[:, 4:5], upper[:, :], small[:, 2:3], start=True, stop=True).then_inc(offs, 1)
                pe.matmul(psS[:, 5:6], allone[:, :], small[:, 2:3], start=True, stop=True).then_inc(offs, 1)


def tables(nc, t, m, d, i, spec, table, dstW):
    nm = spec["name"] + "t_"
    rels, row, dc = spec["rels"], spec["row"], spec["dst"]
    xin = m["hN"] if i == 1 else m["xN"]
    with ExitStack() as ctx:
        def sb(name, shape, dt=F32):
            return ctx.enter_context(nc.sbuf_tensor(nm + name, shape, dt))

        def sem(name):
            return stage_sem(nc, ctx, nm + name)

        xT = sb("xT", [D + 1, K * P])
        dstN = sb("dstN", [P, K, dc])
        dstF = sb("dstF", [P, K, dc])
        st = [sb(f"st{s}", [P, rels, row]) for s in range(2)]
        WR = {0: 64, 1: 64, 2: 68, 3: 512, 4: 512}[i]
        wA = sb("wA", [D + 1, WR])
        wD = sb("wD", [D + 1, dc])
        psA = [ctx.enter_context(nc.psum_tensor(f"{nm}psA{s}", [P, 512], F32)) for s in range(2)]
        psB = [ctx.enter_context(nc.psum_tensor(f"{nm}psB{s}", [P, 512], F32)) for s in range(2)]
        psD = [ctx.enter_context(nc.psum_tensor(f"{nm}psD{s}", [P, 512], F32)) for s in range(2)]
        psX = [ctx.enter_context(nc.psum_tensor(f"{nm}psX{s}", [P, 512], F32)) for s in range(2)]
        loaded, turned, copied, ready, prod, tookV, tookA, scat, back, wch, wpe, xch, ruled = (
            sem(n) for n in ("loaded", "turned", "copied", "ready", "prod", "tookV", "tookA", "scat", "back", "wch", "wpe", "xch", "ruled"))
        put = [sem(f"put{s}") for s in range(2)]
        if i == 0:
            wS = sb("wS", [D + 1, D])
        if i == 2:
            wT = sb("wT", [D, D])
            att = sb("att", [D, 8])
        if i >= 3:
            wB = sb("wB", [D + 1, 512])
            w0 = sb("w0", [D, D])
            w1 = sb("w1", [D, D])
            rowA = sb("rowA", [D + 1, 512])
            rowB = sb("rowB", [D + 1, 512])
        if i == 3:
            rm = sb("rm", [D, REL])
            w2 = sb("w2", [D, D])
            ids = sb("ids", [4, 1], I32)
            rule = sb("rule", [4, D])
            ruleT = sb("ruleT", [D, 4])
            keyT = sb("keyT", [D, 4])
            wqT = sb("wqT", [D, D + 1])
        if i == 4:
            wE = sb("wE", [D + 1, REL * 4])
            eg = sb("eg", [D + 1, REL * 4])
            es = sb("es", [D + 1, REL * 4])
        nload = {0: 3, 1: 2, 2: 3, 3: 8, 4: 9}[i]

        with nc.Block() as block:
            @block.sync
            def _(sp):
                def ld(dst, src):
                    sp.dma_start(dst, src).then_inc(loaded, 16)
                if i in (0, 1):
                    ld(wA[:, :], t[f"Wl{i + 1}"])
                    ld(wD[:, :], t[f"Wr{i + 1}"])
                    if i == 0:
                        ld(wS[:, :], t["Wskip"])
                if i == 2:
                    ld(wA[0:D, 0:D], t["gatW"])
                    ld(wT[:, :], t["gatWT"])
                    ld(att[:, :], t["gatAtt"])
                if i == 3:
                    ld(wB[0:D, :], t["Wrel"])
                    ld(w0[:, :], t["Wk"][0:D, :])
                    ld(w1[:, :], t["Wk"][D:2 * D, :])
                    ld(w2[:, :], t["Wk"][2 * D:3 * D, :])
                    ld(wD[:, 0:D], t["Wq2"])
                    ld(wqT[:, :], t["Wq2T"])
                    ld(rowA[D:D + 1, :].rearrange("a (r f) -> a r f", f=D), over(t["bk2"].rearrange("(a f) -> a f", a=1), 1, [1, REL, D]))
                    ld(ids[:, :], t["ruleids"].rearrange("(r a) -> r a", a=1))
                if i == 4:
                    ld(w0[:, :], t["Wk3"])
                    ld(w1[:, :], t["Wv3"])
                    ld(wD[:, :], t["Wq3"])
                    ld(rowA[D:D + 1, :].rearrange("a (r f) -> a r f", f=D), over(t["bk3"].rearrange("(a f) -> a f", a=1), 1, [1, REL, D]))
                    ld(rowB[D:D + 1, :].rearrange("a (r f) -> a r f", f=D), over(t["bv3"].rearrange("(a f) -> a f", a=1), 1, [1, REL, D]))
                    ld(wA[D:D + 1, :], t["ek"].rearrange("(a r) f -> a (r f)", a=1))
                    ld(wB[D:D + 1, :], t["ev"].rearrange("(a r) f -> a (r f)", a=1))
                    ld(es[D:D + 1, :], t["es"].rearrange("(a r) f -> a (r f)", a=1))
                    ld(eg[D:D + 1, :], t["eg"].rearrange("(a r) f -> a (r f)", a=1))
                rows = table.rearrange("(p k r) c -> p k (r c)", k=K, r=rels)

                def put_rows(k, s):
                    sp.wait_ge(tookV, k + 1)
                    sp.wait_ge(tookA, k + 1)
                    sp.dma_start(rows[:, bass.ds(k, 1), :], st[s][:, :, :].rearrange("p (a r) c -> p a (r c)", a=1)).then_inc(put[s], 16)
                each(sp, K, put_rows)
                sp.wait_ge(put[0], 16 * ((K + 1) // 2))
                sp.wait_ge(put[1], 16 * (K // 2))
                sp.wait_ge(scat, 16 * K)
                sp.dma_start(dstF[:, :, :], d["dst"].rearrange("(w p) c -> p w c", p=P)).then_inc(back, 16)
                sp.wait_ge(back, 16)

            @block.gpsimd
            def _(g):
                g.memset(dstW[:, :, K:WINS, :], 0.0).then_inc(xch, 1)
                if i == 3:
                    g.wait_ge(loaded, 16 * nload)
                    g.indirect_dma_start(rule[:, :], None, t["ruleemb"],
                                         bass.IndirectOffsetOnAxis(ap=ids[:, :].bitcast(U32), axis=0)).then_inc(ruled, 16)
                for k in range(K):
                    g.wait_ge(tookA, k + 1)
                    g.indirect_dma_start(d["dst"], bass.IndirectOffsetOnAxis(ap=m["perm"][:, k:k + 1].bitcast(U32), axis=0),
                                         dstN[:, k, :], None).then_inc(scat, 16)

            @block.vector
            def _(v):
                link = Chain(v, wch)
                v.memset(xT[D:D + 1, :], 1.0).then_inc(xch, 1)
                for c in range(-(-K // 4)):
                    n = min(4, K - 4 * c)
                    v.wait_ge(turned, c + 1)
                    v.tensor_copy(xT[0:D, c * 4 * P:(c * 4 + n) * P], psX[c % 2][0:D, 0:n * P]).then_inc(copied, 1)
                v.wait_ge(loaded, 16 * nload)
                if i == 2:
                    link(v.memset(wA[D:D + 1, :], 0.0))
                    link(v.memset(wD[D:D + 1, :], 0.0))
                    v.wait_ge(wpe, 1)
                    link(v.tensor_copy(wA[0:D, D:D + 4], psA[0][0:D, 0:4]))
                    link(v.tensor_copy(wD[0:D, :], psA[0][0:D, 4:8]))
                if i >= 3:
                    link(v.tensor_copy(wA[0:D, :].rearrange("p (r f) -> p r f", f=D), over(w0[:, :], 1, [D, REL, D])))
                if i == 3:
                    link(v.memset(wB[D:D + 1, :], 0.0))
                    link(v.tensor_reduce(rm[:, :], wB[0:D, :].rearrange("p (r f) -> p r f", f=D), AX_X, ALU.add))
                    v.tensor_scalar(rm[:, :], rm[:, :], 1.0 / D, None, ALU.mult).then_inc(ready, 1)
                    v.wait_ge(wpe, 1)
                    link(v.tensor_copy(ruleT[:, :], psB[0][0:D, 0:4]))
                    link(v.tensor_tensor(wA[D:D + 1, :], psA[0][D:D + 1, :], rowA[D:D + 1, :], ALU.add))
                    v.sem_inc(ready, 1)
                    v.wait_ge(wpe, 2)
                    link(v.tensor_copy(keyT[:, :], psB[0][0:D, 8:12]))
                    v.sem_inc(ready, 1)
                    v.wait_ge(wpe, 3)
                    link(v.tensor_copy(wD[:, D:D + 4], psB[0][0:D + 1, 16:20]))
                if i == 4:
                    link(v.tensor_copy(wB[0:D, :].rearrange("p (r f) -> p r f", f=D), over(w1[:, :], 1, [D, REL, D])))
                    link(v.tensor_tensor(wA[D:D + 1, :], wA[D:D + 1, :], rowA[D:D + 1, :], ALU.add))
                    link(v.tensor_tensor(wB[D:D + 1, :], wB[D:D + 1, :], rowB[D:D + 1, :], ALU.add))
                    link(v.memset(wE[0:D, :], 0.0))
                    v.wait_ge(wpe, 1)
                    link(v.tensor_scalar(eg[D:D + 1, :], eg[D:D + 1, :], 10.0, -10.0, ALU.min, ALU.max))
                    link(v.tensor_tensor(wE[D:D + 1, :], eg[D:D + 1, :], es[D:D + 1, :], ALU.add))
                v.sem_inc(ready, 1)

                def take(k, s):
                    v.wait_ge(prod, k + 1)
                    wait(v, put[s], (k - s) * 8)
                    if i <= 2:
                        v.tensor_copy(st[s][:, 0, :], psA[s][:, 0:row]).then_inc(tookV, 1)
                    else:
                        v.tensor_copy(st[s][:, :, 0:D], psA[s][:, :].rearrange("p (r f) -> p r f", f=D)).then_inc(tookV, 1)
                each(v, K, take)
                v.wait_ge(back, 16)
                for part in range(3):
                    link(v.tensor_copy(dstW[:, part, 0:K, :], dstF[:, :, :]))
                    if part < 2:
                        link(v.tensor_tensor(dstF[:, :, :], dstF[:, :, :], dstW[:, part, 0:K, :], ALU.subtract))

            @block.scalar
            def _(a):
                if i == 4:
                    a.wait_ge(loaded, 16 * nload)
                    a.activation(eg[D:D + 1, :], eg[D:D + 1, :], ACT.Ln).then_inc(wpe, 1)

                def take(k, s):
                    a.wait_ge(prod, k + 1)
                    if i >= 3:
                        wait(a, put[s], (k - s) * 8)
                        a.activation(st[s][:, :, D:2 * D], psB[s][:, :].rearrange("p (r f) -> p r f", f=D), ACT.Copy)
                    if i == 4:
                        a.activation(st[s][:, :, 2 * D:2 * D + 4], psD[s][:, 128:160].rearrange("p (r h) -> p r h", h=4), ACT.Copy)
                    if i == 0:
                        a.activation(m["skipN"][:, bass.ds(k, 1), :], psD[s][:, 128:192].rearrange("p (a f) -> p a f", a=1), ACT.Copy)
                    a.activation(dstN[:, bass.ds(k, 1), :], psD[s][:, 0:dc].rearrange("p (a f) -> p a f", a=1), ACT.Copy).then_inc(tookA, 1)
                each(a, K, take)

            @block.tensor
            def _(pe):
                for c in range(-(-K // 4)):
                    if c >= 2:
                        pe.wait_ge(copied, c - 1)
                    for k in range(4 * c, min(4 * c + 4, K)):
                        last = pe.transpose(psX[c % 2][0:D, (k % 4) * P:(k % 4 + 1) * P], xin[:, k, :], m["ident"][:, :])
                    last.then_inc(turned, 1)
                if i == 2:
                    pe.wait_ge(loaded, 16 * nload)
                    pe.matmul(psA[0][0:D, 0:8], wT[:, :], att[:, :], start=True, stop=True).then_inc(wpe, 1)
                if i == 3:
                    pe.wait_ge(ready, 1)
                    pe.wait_ge(ruled, 16)
                    for r in range(REL):
                        pe.matmul(psA[0][D:D + 1, r * D:(r + 1) * D], rm[:, r:r + 1], w1[:, :], start=True, stop=True)
                    pe.transpose(psB[0][0:D, 0:4], rule[:, :], m["ident"][0:4, 0:4]).then_inc(wpe, 1)
                    pe.wait_ge(ready, 2)
                    pe.matmul(psB[0][0:D, 8:12], w2[:, :], ruleT[:, :], start=True, stop=True).then_inc(wpe, 1)
                    pe.wait_ge(ready, 3)
                    pe.matmul(psB[0][0:D + 1, 16:20], wqT[:, :], keyT[:, :], start=True, stop=True).then_inc(wpe, 1)
                pe.wait_ge(xch, 2)
                pe.wait_ge(copied, -(-K // 4))
                pe.wait_ge(ready, 4 if i == 3 else 1)

                def products(k, s):
                    wait(pe, tookV, k - 1)
                    wait(pe, tookA, k - 1)
                    x = xT[:, k * P:(k + 1) * P]
                    pe.matmul(psA[s][:, 0:WR], x, wA[:, :], start=True, stop=True)
                    if i >= 3:
                        pe.matmul(psB[s][:, :], x, wB[:, :], start=True, stop=True)
                    if i == 4:
                        pe.matmul(psD[s][:, 128:160], x, wE[:, :], start=True, stop=True)
                    if i == 0:
                        pe.matmul(psD[s][:, 128:192], x, wS[:, :], start=True, stop=True)
                    pe.matmul(psD[s][:, 0:dc], x, wD[:, :], start=True, stop=True).then_inc(prod, 1)
                for k in range(K):
                    products(k, k % 2)


def scores(nc, t, m, d, i, spec, table, dstW):
    nm = spec["name"] + "s_"
    row, msg, dc, H = spec["row"], spec["msg"], spec["dst"], spec["heads"]
    idx = m["srcI"] if i <= 2 else m["typedI"]
    relrow = d["rel"].rearrange("(a r) e -> a (r e)", a=1)
    with ExitStack() as ctx:
        def sb(name, shape, dt=F32):
            return ctx.enter_context(nc.sbuf_tensor(nm + name, shape, dt))

        def sem(name):
            return stage_sem(nc, ctx, nm + name)

        GE = GROUP * P
        gat = [sb(f"gat{s}", [P, GROUP, row]) for s in range(RING)]
        idxS = [sb(f"idx{s}", [P, GROUP], I32) for s in range(RING)]
        rank = [sb(f"rank{s}", [1, GE], BF16) for s in range(RING)]
        hot = [sb(f"hot{s}", [P, 2, GE], BF16) for s in range(2)]
        mid = [sb(f"mid{s}", [P, GROUP, D]) for s in range(2)]
        act = [sb(f"act{s}", [P, GROUP, D]) for s in range(2)]
        red = [sb(f"red{s}", [P, GROUP, 4]) for s in range(2)]
        if i <= 1:
            ea = [sb(f"ea{s}", [D, GE]) for s in range(RING)]
            we = sb("we", [D, D])
        DW = 64 if i <= 2 else 128
        psR = [ctx.enter_context(nc.psum_tensor(f"{nm}psR{s}", [P, GE], F32)) for s in range(2)]
        psM = [ctx.enter_context(nc.psum_tensor(f"{nm}psM{s}", [P, GROUP * DW], F32)) for s in range(2)]
        staged, spread, hots, made, used, ch, pch, wl = (
            sem(n) for n in ("staged", "spread", "hots", "made", "used", "ch", "pch", "wl"))
        got = [sem(f"got{s}") for s in range(RING)]
        spilt = [sem(f"spilt{s}") for s in range(RING)]
        fed = [sem(f"fed{s}") for s in range(RING)]
        FEED = 32 if i <= 1 else 16

        with nc.Block() as block:
            @block.sync
            def _(sp):
                if i <= 1:
                    sp.dma_start(we[:, :], t[f"We{i + 1}"]).then_inc(wl, 16)

                def feed(g, s):
                    wait(sp, made, g - RING + 1)
                    sp.dma_start(rank[s][:, :], relrow[:, bass.ds(g * GE, GE)]).then_inc(fed[s], 16)
                    if i <= 1:
                        sp.dma_start(ea[s][:, :], t["eaT"][:, bass.ds(g * GE, GE)]).then_inc(fed[s], 16)
                each(sp, GROUPS, feed, RING)

            @block.scalar
            def _(a):
                def stage(g, s):
                    wait(a, got[s], (g - s) * (GOT // RING))
                    a.activation(idxS[s][:, :], idx[:, bass.ds(g * GROUP, GROUP)], ACT.Copy).then_inc(staged, 1)

                def step(g, s):
                    if not isinstance(g, int) or g < GROUPS - 1:
                        stage(g + 1, (s + 1) % RING)
                    a.wait_ge(got[s], (g - s) * (GOT // RING) + GOT)
                    a.dma_start(d["spill"][:, bass.ds(g * GROUP, GROUP), :], gat[s][:, :, msg:msg + D]).then_inc(spilt[s], 16)
                stage(0, 0)
                each(a, GROUPS, step, RING)
                for s in range(RING):
                    a.wait_ge(spilt[s], 16 * (GROUPS // RING))

            @block.gpsimd
            def _(g_):
                def gather(g, s):
                    g_.wait_ge(staged, g + 1)
                    wait(g_, used, g - RING + 1)
                    wait(g_, spilt[s], (g - s) * (16 // RING))
                    g_.sem_inc(pch, 1)
                    for j in range(GROUP):
                        g_.indirect_dma_start(gat[s][:, j, :], None, table,
                                              bass.IndirectOffsetOnAxis(ap=idxS[s][:, j:j + 1].bitcast(U32), axis=0)).then_inc(got[s], 16)
                each(g_, GROUPS, gather, RING)

            @block.vector
            def _(v):
                def onehot(g, s):
                    h = s % 2
                    v.wait_ge(spread, g + 1)
                    wait(v, made, g - 1)
                    for a in range(2):
                        v.tensor_scalar(hot[h][:, a, :], psR[h][:, :], m["pid"][:, a:a + 1], None, ALU.is_equal).then_inc(hots, 1)

                LINKS = {0: 3, 1: 3, 2: 1, 3: 2, 4: 2}[i]

                def score(g, s):
                    k = [0]

                    def link(ins):
                        k[0] += 1
                        ins.then_inc(ch, 1)
                        v.wait_ge(ch, g * LINKS + k[0])

                    v.wait_ge(made, g + 1)
                    v.wait_ge(got[s], (g - s) * (GOT // RING) + GOT)
                    dst3 = psM[s % 2][:, :].rearrange("p (j c) -> p j c", c=DW)
                    outp = m["score"][:, :, bass.ds(g * GROUP, GROUP)].rearrange("p h j -> p j h")
                    if i <= 1:
                        link(v.tensor_tensor(mid[s % 2][:, :, :], dst3, gat[s][:, :, :], ALU.add))
                        link(v.scalar_tensor_tensor(act[s % 2][:, :, :], mid[s % 2][:, :, :], 0.2, mid[s % 2][:, :, :], ALU.mult, ALU.max))
                        link(v.tensor_tensor(mid[s % 2][:, :, :], act[s % 2][:, :, :], over(m["vec"][:, VECS.index(f"att{i + 1}"), :], 1, [P, GROUP, D]), ALU.mult))
                        v.tensor_reduce(m["score"][:, 0, bass.ds(g * GROUP, GROUP)], mid[s % 2][:, :, :], AX_X, ALU.add).then_inc(used, 1)
                    elif i == 2:
                        link(v.tensor_tensor(red[s % 2][:, :, :], dst3[:, :, 0:4], gat[s][:, :, D:D + 4], ALU.add))
                        v.scalar_tensor_tensor(outp, red[s % 2][:, :, :], 0.2, red[s % 2][:, :, :], ALU.mult, ALU.max).then_inc(used, 1)
                    elif i == 3:
                        link(v.tensor_tensor(mid[s % 2][:, :, :], dst3[:, :, 0:D], gat[s][:, :, 0:D], ALU.mult))
                        link(v.tensor_reduce(red[s % 2][:, :, 0:1], mid[s % 2][:, :, :], AX_X, ALU.add))
                        v.tensor_tensor(outp, dst3[:, :, D:D + 4], red[s % 2][:, :, 0:1].broadcast_to([P, GROUP, 4]), ALU.add).then_inc(used, 1)
                    else:
                        link(v.tensor_tensor(mid[s % 2][:, :, :], dst3[:, :, 0:D], gat[s][:, :, 0:D], ALU.mult))
                        link(v.tensor_reduce(red[s % 2][:, :, :], mid[s % 2][:, :, :].rearrange("p j (h c) -> p j h c", h=4), AX_X, ALU.add))
                        v.scalar_tensor_tensor(outp, red[s % 2][:, :, :], 0.25, gat[s][:, :, 2 * D:2 * D + 4], ALU.mult, ALU.add).then_inc(used, 1)

                def step(g, s):
                    if not isinstance(g, int) or g < GROUPS - 1:
                        onehot(g + 1, (s + 1) % RING)
                    score(g, s)
                onehot(0, 0)
                each(v, GROUPS, step, RING)

            @block.tensor
            def _(pe):
                def spread_ranks(g, s):
                    pe.wait_ge(fed[s], (g - s) * (FEED // RING) + FEED)
                    wait(pe, hots, g * 2 - 2)
                    for c in range(2):
                        last = pe.matmul(psR[s % 2][:, c * 512:(c + 1) * 512], m["onesB"][:, :], rank[s][:, c * 512:(c + 1) * 512],
                                         start=True, stop=True)
                    last.then_inc(spread, 1)

                def step(g, s):
                    if not isinstance(g, int) or g < GROUPS - 1:
                        spread_ranks(g + 1, (s + 1) % RING)
                    windows = load_windows(nc, m, g)
                    pe.wait_ge(hots, g * 2 + 2)
                    wait(pe, used, g - 1)
                    for j in range(GROUP):
                        w = windows[j]
                        o = psM[s % 2][:, j * DW:j * DW + dc]
                        for a in range(2):
                            for part in range(3):
                                last = pe.matmul(o, hot[s % 2][:, a, j * P:(j + 1) * P], dstAt[a][part][:, bass.ds(w, 1), :],
                                                 start=(a == part == 0), stop=(a == 1 and part == 2 and i > 1))
                        if i <= 1:
                            last = pe.matmul(o, ea[s][:, j * P:(j + 1) * P], we[:, :], start=False, stop=True)
                    last.then_inc(made, 1)
                dstF = dstW[:, :, :, :].rearrange("p t w f -> p (t w f)")
                dstAt = [[dstF[:, (part * WINS + a) * dc:(part * WINS + a + K) * dc].rearrange("p (w f) -> p w f", f=dc)
                          for part in range(3)] for a in range(2)]
                if i <= 1:
                    pe.wait_ge(wl, 16)
                spread_ranks(0, 0)
                each(pe, GROUPS, step, RING)


def softmax(nc, m, i, spec):
    nm = spec["name"] + "x_"
    H = spec["heads"]
    with ExitStack() as ctx:
        def sb(name, shape, dt=F32):
            return ctx.enter_context(nc.sbuf_tensor(nm + name, shape, dt))

        def sem(name):
            return stage_sem(nc, ctx, nm + name)

        X = sb("X", [ROWS, H, L])
        A = sb("A", [ROWS, H, L])
        B = sb("B", [ROWS, H, L])
        pen = sb("pen", [ROWS, L], BF16)
        pen2 = sb("pen2", [ROWS, L], BF16)
        ends = sb("ends", [ROWS, 8])
        endT = sb("endT", [8, ROWS + 2])
        carr = sb("carr", [8, 2, ROWS])
        lnk = sb("lnk", [8, ROWS])
        tk = sb("tk", [8, ROWS])
        carry = sb("carry", [ROWS, 16])
        psT = [ctx.enter_context(nc.psum_tensor(f"{nm}psT{s}", [P, 512], F32)) for s in range(2)]
        psE = ctx.enter_context(nc.psum_tensor(f"{nm}psE", [P, 512], F32))
        turned, copied, ch, want, gave, sub, exped, wback, returned, normed = (
            sem(n) for n in ("turned", "copied", "ch", "want", "gave", "sub", "exped", "wback", "returned", "normed"))
        scoreT = m["score"][:, :, :].rearrange("p h (r b) -> p h r b", b=BLK)
        HOUT = 1 if i == 3 else H
        blocks = [(b, min(4, BLK - b)) for b in range(0, BLK, 4)]
        steps = [(h, b, n) for h in range(H) for b, n in blocks]
        osteps = [(h, b, n) for h in range(HOUT) for b, n in blocks]

        with nc.Block() as block:
            @block.scalar
            def _(a):
                for c, (h, b, n) in enumerate(steps):
                    a.wait_ge(turned, c + 1)
                    a.activation(X[:, h, b * P:(b + n) * P], psT[c % 2][0:ROWS, 0:n * P], ACT.Copy, scale=spec["scale"]).then_inc(copied, 1)
                for h in range(H):
                    a.wait_ge(sub, h + 1)
                    a.activation(X[:, h, :], X[:, h, :], ACT.Exp).then_inc(exped, 1)
                for c, (h, b, n) in enumerate(osteps):
                    a.wait_ge(returned, c + 1)
                    a.activation(scoreT[:, h, :, b:b + n], psT[c % 2][:, 0:n * ROWS].rearrange("p (b r) -> p r b", b=n),
                                 ACT.Copy).then_inc(wback, 1)

            @block.tensor
            def _(pe):
                for c, (h, b, n) in enumerate(steps):
                    if c >= 2:
                        pe.wait_ge(copied, c - 1)
                    for q in range(n):
                        last = pe.transpose(psT[c % 2][0:ROWS, q * P:(q + 1) * P], scoreT[:, h, :, b + q], m["ident"][:, :])
                    last.then_inc(turned, 1)
                for q in range(2):
                    pe.wait_ge(want, 2 * q + 1)
                    pe.transpose(psE[0:8, 0:ROWS], ends[:, :], m["ident"][0:ROWS, 0:ROWS]).then_inc(gave, 1)
                    pe.wait_ge(want, 2 * q + 2)
                    for x in range(2):
                        last = pe.transpose(psE[0:ROWS, 128 + 8 * x:136 + 8 * x], carr[:, x, :], m["ident"][0:8, 0:8])
                    last.then_inc(gave, 1)
                pe.wait_ge(copied, len(steps))
                for c, (h, b, n) in enumerate(osteps):
                    pe.wait_ge(normed, h + 1)
                    if c >= 2:
                        pe.wait_ge(wback, c - 1)
                    for q in range(n):
                        last = pe.transpose(psT[c % 2][:, q * ROWS:(q + 1) * ROWS], X[:, h, (b + q) * P:(b + q + 1) * P],
                                            m["ident"][0:ROWS, 0:ROWS])
                    last.then_inc(returned, 1)

            @block.vector
            def _(v):
                link = Chain(v, ch)

                def segments(q, biggest):
                    if biggest:
                        link(v.tensor_scalar(pen[:, :], m["contP"][:, :], BIG, -BIG, ALU.mult, ALU.add))
                        link(v.tensor_scalar(pen2[:, :], m["contN"][:, :], BIG, -BIG, ALU.mult, ALU.add))
                    for h in range(H):
                        if biggest:
                            v.wait_ge(copied, len(blocks) * (h + 1))
                            link(v.tensor_tensor_scan(A[:, h, :], pen[:, :], X[:, h, :], -BIG, ALU.add, ALU.max))
                            link(v.tensor_tensor_scan(B[:, h, ::-1], pen2[:, ::-1], A[:, h, ::-1], -BIG, ALU.add, ALU.max))
                        else:
                            v.wait_ge(exped, h + 1)
                            link(v.tensor_tensor_scan(A[:, h, :], m["contP"][:, :], X[:, h, :], 0.0, ALU.mult, ALU.add))
                            link(v.tensor_tensor(A[:, h, :], A[:, h, :], pen2[:, :], ALU.mult))
                            link(v.tensor_tensor_scan(B[:, h, ::-1], m["contN"][:, ::-1], A[:, h, ::-1], 0.0, ALU.mult, ALU.add))
                    link(v.memset(ends[:, :], 0.0))
                    link(v.tensor_copy(ends[:, 0:H], B[:, :, 0]))
                    v.tensor_copy(ends[:, 4:4 + H], B[:, :, L - 1]).then_inc(want, 1)
                    v.wait_ge(gave, 2 * q + 1)
                    link(v.memset(endT[:, :], 0.0))
                    link(v.tensor_copy(endT[:, 1:ROWS + 1], psE[0:8, 0:ROWS]))
                    for x, (link_, take, lo, rev) in enumerate(((m["linkF"], m["takeF"], 0, 1), (m["linkB"], m["takeB"], 2, -1))):
                        nb = endT[:, lo:lo + ROWS]
                        if biggest:
                            link(v.tensor_scalar(lnk[:, :], link_[:, :], BIG, -BIG, ALU.mult, ALU.add))
                            link(v.tensor_scalar(tk[:, :], take[:, :], BIG, -BIG, ALU.mult, ALU.add))
                            link(v.tensor_tensor(tk[:, :], tk[:, :], nb, ALU.add))
                            link(v.tensor_tensor_scan(carr[:, x, ::rev], lnk[:, ::rev], tk[:, ::rev], -BIG, ALU.add, ALU.max))
                        else:
                            link(v.tensor_tensor(tk[:, :], take[:, :], nb, ALU.mult))
                            link(v.tensor_tensor_scan(carr[:, x, ::rev], link_[:, ::rev], tk[:, ::rev], 0.0, ALU.mult, ALU.add))
                    v.sem_inc(want, 1)
                    v.wait_ge(gave, 2 * q + 2)
                    link(v.tensor_copy(carry[:, :], psE[0:ROWS, 128:144]))
                    for mask, at in ((m["first"], 4), (m["last"], 8)):
                        if biggest:
                            link(v.tensor_scalar(pen[:, :], mask[:, :], BIG, -BIG, ALU.mult, ALU.add))
                        for h in range(H):
                            c = carry[:, at + h:at + h + 1]
                            if biggest:
                                link(v.scalar_tensor_tensor(B[:, h, :], pen[:, :], c, B[:, h, :], ALU.add, ALU.max))
                            else:
                                link(v.scalar_tensor_tensor(B[:, h, :], mask[:, :], c, B[:, h, :], ALU.mult, ALU.add))

                segments(0, True)
                for h in range(H):
                    v.tensor_tensor(X[:, h, :], X[:, h, :], B[:, h, :], ALU.subtract).then_inc(sub, 1)
                link(v.tensor_scalar(pen2[:, :], m["contN"][:, :], -1.0, 1.0, ALU.mult, ALU.add))
                link(v.memset(pen2[:, L - 1:L], 1.0))
                segments(1, False)
                for h in range(H):
                    if i == 4:
                        link(v.tensor_scalar_max(B[:, h, :], B[:, h, :], 1e-12))
                    elif spec["eps"]:
                        link(v.tensor_scalar_add(B[:, h, :], B[:, h, :], spec["eps"]))
                    link(v.reciprocal(A[:, h, :], B[:, h, :]))
                    if i == 3:
                        link(v.tensor_tensor(X[:, h, :], X[:, h, :], A[:, h, :], ALU.mult))
                    else:
                        v.tensor_tensor(X[:, h, :], X[:, h, :], A[:, h, :], ALU.mult).then_inc(normed, 1)
                if i == 3:
                    link(v.tensor_tensor(A[:, 0, :], X[:, 0, :], X[:, 1, :], ALU.add))
                    link(v.tensor_tensor(A[:, 1, :], X[:, 2, :], X[:, 3, :], ALU.add))
                    link(v.tensor_tensor(A[:, 0, :], A[:, 0, :], A[:, 1, :], ALU.add))
                    v.tensor_scalar(X[:, 0, :], A[:, 0, :], 0.25, None, ALU.mult).then_inc(normed, 1)


def aggregate(nc, m, d, i, spec):
    nm = spec["name"] + "g_"
    H = 1 if i == 3 else spec["heads"]
    with ExitStack() as ctx:
        def sb(name, shape, dt=F32):
            return ctx.enter_context(nc.sbuf_tensor(nm + name, shape, dt))

        def sem(name):
            return stage_sem(nc, ctx, nm + name)

        msgs = [sb(f"msg{s}", [P, GROUP, D]) for s in range(RING)]
        wtd = [sb(f"wtd{s}", [P, GROUP, D]) for s in range(RING)]
        res = [sb(f"res{s}", [P, GROUP, D]) for s in range(RING)]
        parts = [sb(f"parts{s}", [P, 3, GROUP, D], BF16) for s in range(RING)]
        hot = [sb(f"hot{s}", [P, GROUP, 2 * P], BF16) for s in range(RING)]
        zero = sb("zero", [P, 512])
        outS = sb("outS", [P, K, D])
        BANKS = -(-WINS * D // 512)
        psG = ctx.enter_context(nc.psum_tensor(nm + "psG", [P, BANKS * 512], F32))
        zeroed, hots, weighted, high, rest, middle, low, summed, done, copied, stored, pch = (
            sem(n) for n in ("zeroed", "hots", "weighted", "high", "rest", "middle", "low", "summed", "done", "copied", "stored", "pch"))
        fed = [sem(f"fed{s}") for s in range(RING)]

        def there(g):
            return not isinstance(g, int) or g < GROUPS

        with nc.Block() as block:
            @block.sync
            def _(sp):
                def feed(g, s):
                    wait(sp, weighted, g - RING + 1)
                    sp.dma_start(msgs[s][:, :, :], d["spill"][:, bass.ds(g * GROUP, GROUP), :]).then_inc(fed[s], 16)
                each(sp, GROUPS, feed, RING)
                sp.wait_ge(copied, 1)
                sp.dma_start(d["agg"].rearrange("(w p) f -> p w f", p=P), outS[:, :, :]).then_inc(stored, 16)
                sp.wait_ge(stored, 16)

            @block.gpsimd
            def _(gp):
                def weigh(g, s):
                    gp.wait_ge(fed[s], (g - s) * (16 // RING) + 16)
                    wait(gp, rest, g - RING + 1)
                    gp.sem_inc(pch, 1)
                    if H == 1:
                        gp.tensor_tensor(wtd[s][:, :, :], msgs[s][:, :, :],
                                         over(m["score"][:, 0, bass.ds(g * GROUP, GROUP)], 2, [P, GROUP, D]), ALU.mult).then_inc(weighted, 1)
                    else:
                        al = m["score"][:, :, bass.ds(g * GROUP, GROUP)].rearrange("p h j -> p j h")
                        gp.tensor_tensor(wtd[s][:, :, :].rearrange("p j (h c) -> p j h c", h=4),
                                         msgs[s][:, :, :].rearrange("p j (h c) -> p j h c", h=4),
                                         over(al, 3, [P, GROUP, 4, D // 4]), ALU.mult).then_inc(weighted, 1)

                def step(g, s):
                    if there(g + 3):
                        weigh(g + 3, (s + 3) % RING)
                    gp.wait_ge(middle, g + 1)
                    gp.tensor_tensor(parts[s][:, 2, :, :], res[s][:, :, :], parts[s][:, 1, :, :], ALU.subtract).then_inc(low, 1)
                for g in range(3):
                    weigh(g, g)
                each(gp, GROUPS, step, RING)

            @block.scalar
            def _(a):
                def take_high(g, s):
                    a.wait_ge(weighted, g + 1)
                    wait(a, summed, g - RING + 1)
                    a.activation(parts[s][:, 0, :, :], wtd[s][:, :, :], ACT.Copy).then_inc(high, 1)

                def take_middle(g, s):
                    a.wait_ge(rest, g + 1)
                    a.activation(parts[s][:, 1, :, :], res[s][:, :, :], ACT.Copy).then_inc(middle, 1)

                def step(g, s):
                    if there(g + 2):
                        take_high(g + 2, (s + 2) % RING)
                    if there(g + 1):
                        take_middle(g + 1, (s + 1) % RING)
                take_high(0, 0)
                take_high(1, 1)
                take_middle(0, 0)
                each(a, GROUPS, step, RING)

            @block.vector
            def _(v):
                v.memset(zero[:, :], 0.0).then_inc(zeroed, 1)

                def remainder(g, s):
                    v.wait_ge(high, g + 1)
                    wait(v, low, g - RING + 1)
                    v.tensor_tensor(res[s][:, :, :], wtd[s][:, :, :], parts[s][:, 0, :, :], ALU.subtract).then_inc(rest, 1)

                def onehot(g, s):
                    wait(v, summed, g - RING + 1)
                    for j in range(GROUP):
                        last = v.tensor_scalar(hot[s][:, j, :], m["iotaB"][:, :], m["rel"][:, bass.ds(g * GROUP + j, 1)], None, ALU.is_equal)
                    last.then_inc(hots, 1)

                def step(g, s):
                    if there(g + 1):
                        remainder(g + 1, (s + 1) % RING)
                        onehot(g + 1, (s + 1) % RING)
                remainder(0, 0)
                onehot(0, 0)
                each(v, GROUPS, step, RING)
                v.wait_ge(done, 1)
                v.tensor_copy(outS[:, :, :].rearrange("p w f -> p (w f)"), psG[:, 0:K * D]).then_inc(copied, 1)

            @block.tensor
            def _(pe):
                windows3 = [psG[:, a * D:(a + K) * D].rearrange("p (w f) -> p w f", f=D) for a in range(2)]
                pe.wait_ge(zeroed, 1)
                for b in range(BANKS):
                    pe.matmul(psG[:, b * 512:(b + 1) * 512], zero[:, 0:P], zero[:, :], start=True, stop=False, skip_group_check=True)

                def step(g, s):
                    windows = load_windows(nc, m, g)
                    pe.wait_ge(hots, g + 1)
                    pe.wait_ge(low, g + 1)
                    for j in range(GROUP):
                        w = windows[j]
                        for a in range(2):
                            for part in range(3):
                                last = pe.matmul(windows3[a][:, bass.ds(w, 1), :], hot[s][:, j, a * P:(a + 1) * P], parts[s][:, part, j, :],
                                                 start=False, stop=False, skip_group_check=True)
                    last.then_inc(summed, 1)
                each(pe, GROUPS, step, RING)
                for b in range(BANKS):
                    last = pe.matmul(psG[:, b * 512:(b + 1) * 512], zero[:, 0:P], zero[:, :], start=False, stop=True, skip_group_check=True)
                last.then_inc(done, 1)


def finish(nc, t, m, d, i, spec):
    nm = spec["name"] + "f_"
    with ExitStack() as ctx:
        def sb(name, shape, dt=F32):
            return ctx.enter_context(nc.sbuf_tensor(nm + name, shape, dt))

        def sem(name):
            return stage_sem(nc, ctx, nm + name)

        Y = sb("Y", [P, K, D])
        Q = sb("Q", [P, K, D])
        mean = sb("mean", [P, K])
        var = sb("var", [P, K])
        rstd = sb("rstd", [P, K])
        eps = sb("eps", [P, 1])
        ch, asked, rooted, loaded, turned, copied, proj, took, act = (
            sem(n) for n in ("ch", "asked", "rooted", "loaded", "turned", "copied", "proj", "took", "act"))
        spans = [(0, K)] if i == 4 else [(0, K // 3), (K // 3, 2 * K // 3), (2 * K // 3, K)]
        got = [sem(f"got{c}") for c in range(len(spans))]
        if i == 4:
            xT = sb("xT", [P, K * P])
            x1 = sb("x1", [P, K, D])
            hid = [sb(f"hid{s}", [P, P]) for s in range(2)]
            wO = sb("wO", [D, D])
            w1 = sb("w1", [D + 1, 2 * D])
            w2 = sb("w2", [2 * D, D])
            wf = sb("wf", [D + 1, 2 * D])
            task = sb("task", [D + 1, P])
            gb = sb("gb", [P, 2 * D])
            psX = [ctx.enter_context(nc.psum_tensor(f"{nm}psX{s}", [P, 512], F32)) for s in range(2)]
            psP = [ctx.enter_context(nc.psum_tensor(f"{nm}psP{s}", [P, 512], F32)) for s in range(2)]
            psF = ctx.enter_context(nc.psum_tensor(f"{nm}psF", [P, 512], F32))
        NC = -(-K // 4)

        with nc.Block() as block:
            @block.gpsimd
            def _(g):
                for c, (lo, hi) in enumerate(spans):
                    for k in range(lo, hi):
                        g.indirect_dma_start(Y[:, k, :], None, d["agg"],
                                             bass.IndirectOffsetOnAxis(ap=m["perm"][:, k:k + 1].bitcast(U32), axis=0)).then_inc(got[c], 16)

            if i == 4:
                @block.sync
                def _(sp):
                    sp.dma_start(wO[:, :], t["Wo3"]).then_inc(loaded, 16)
                    sp.dma_start(w1[:, :], t["W1"]).then_inc(loaded, 16)
                    sp.dma_start(w2[:, :], t["W2"]).then_inc(loaded, 16)
                    sp.dma_start(wf[:, :], t["Wf"]).then_inc(loaded, 16)
                    sp.dma_start(task[:, :], t["task"]).then_inc(loaded, 16)

                @block.tensor
                def _(pe):
                    pe.wait_ge(loaded, 80)
                    pe.matmul(psF[:, 0:2 * D], task[:, :], wf[:, :], start=True, stop=True).then_inc(proj, 1)

                    def turn(src, base):
                        for c in range(NC):
                            if base + c >= 2:
                                pe.wait_ge(copied, base + c - 1)
                            for k in range(4 * c, min(4 * c + 4, K)):
                                last = pe.transpose(psX[(base + c) % 2][0:D, (k % 4) * P:(k % 4 + 1) * P], src[:, k, :], m["ident"][:, :])
                            last.then_inc(turned, 1)
                    pe.wait_ge(got[0], 16 * K)
                    turn(Y, 0)
                    pe.wait_ge(copied, NC)

                    def outp(k, s):
                        wait(pe, took, k - 1)
                        pe.matmul(psP[s][:, 0:D], xT[0:D, k * P:(k + 1) * P], wO[:, :], start=True, stop=True).then_inc(proj, 1)
                    for k in range(K):
                        outp(k, k % 2)
                    pe.wait_ge(asked, 2)
                    turn(x1, NC)
                    pe.wait_ge(copied, 2 * NC)

                    def hidden(k, s):
                        wait(pe, act, k - 1)
                        pe.matmul(psX[s][:, 0:P], w1[:, :], xT[0:D + 1, bass.ds(k * P, P)], start=True, stop=True).then_inc(turned, 1)

                    def ffn(k, s):
                        if not isinstance(k, int) or k + 1 < K:
                            hidden(k + 1, (s + 1) % 2)
                        pe.wait_ge(act, k + 1)
                        pe.wait_ge(took, k + K - 1)
                        pe.matmul(psP[s][:, 0:D], hid[s][:, :], w2[:, :], start=True, stop=True).then_inc(proj, 1)
                    hidden(0, 0)
                    each(pe, K, ffn)

            @block.scalar
            def _(a):
                n = {0: 1, 1: 2, 2: 2, 3: 2, 4: 1}[i]
                if i == 4:
                    a.wait_ge(proj, 1)
                    a.activation(gb[:, 0:D], psF[:, 0:D], ACT.Tanh).then_inc(rooted, 1)
                    a.wait_ge(asked, 1)
                    a.activation(rstd[:, :], var[:, :], ACT.Sqrt, bias=eps[:, 0:1]).then_inc(rooted, 1)

                    def gelu(k, s):
                        a.wait_ge(turned, k + 2 * NC + 1)
                        wait(a, proj, k + K)
                        a.activation(hid[s][:, :], psX[s][:, 0:P], ACT.Gelu).then_inc(act, 1)
                    each(a, K, gelu)
                    for q in range(2):
                        a.wait_ge(asked, 3 + q)
                        a.activation(rstd[:, :], var[:, :], ACT.Sqrt, bias=eps[:, 0:1]).then_inc(rooted, 1)
                else:
                    for c, (lo, hi) in enumerate(spans):
                        for q in range(n):
                            a.wait_ge(asked, c * n + q + 1)
                            a.activation(rstd[:, lo:hi], var[:, lo:hi], ACT.Sqrt, bias=eps[:, 0:1]).then_inc(rooted, 1)

            @block.vector
            def _(v):
                link = Chain(v, ch)
                roots = [1 if i == 4 else 0]

                def vec(name, n=K):
                    return over(m["vec"][:, VECS.index(name), :], 1, [P, n, D])

                def norm(dst, src, span=(0, K)):
                    s, shape = slice(*span), [P, span[1] - span[0], D]
                    link(v.tensor_reduce(mean[:, s], src[:, s, :], AX_X, ALU.add))
                    link(v.tensor_scalar(mean[:, s], mean[:, s], -1.0 / D, None, ALU.mult))
                    link(v.tensor_tensor(dst[:, s, :], src[:, s, :], over(mean[:, s], 2, shape), ALU.add))
                    link(v.tensor_tensor(Q[:, s, :], dst[:, s, :], dst[:, s, :], ALU.mult))
                    link(v.tensor_reduce(var[:, s], Q[:, s, :], AX_X, ALU.add))
                    v.tensor_scalar(var[:, s], var[:, s], 1.0 / D, None, ALU.mult).then_inc(asked, 1)
                    roots[0] += 1
                    v.wait_ge(rooted, roots[0])
                    link(v.reciprocal(mean[:, s], rstd[:, s]))
                    link(v.tensor_tensor(dst[:, s, :], dst[:, s, :], over(mean[:, s], 2, shape), ALU.mult))

                xN = m["xN"]
                full = [P, K, D]
                link(v.memset(eps[:, :], 1e-5))
                for c, span in enumerate(spans):
                    v.wait_ge(got[c], 16 * (span[1] - span[0]))
                    n, s = span[1] - span[0], slice(*span)
                    y = Y[:, s, :]
                    if i == 0:
                        link(v.tensor_tensor(y, y, vec("bo1", n), ALU.add))
                        link(v.tensor_scalar_max(y, y, 0.0))
                        norm(m["hN"], Y, span)
                    if i == 1:
                        link(v.tensor_tensor(y, y, vec("bo2", n), ALU.add))
                        link(v.tensor_tensor(y, y, m["skipN"][:, s, :], ALU.add))
                        link(v.tensor_scalar_max(y, y, 0.0))
                        norm(Y, Y, span)
                    if i == 2:
                        link(v.tensor_tensor(y, y, vec("bias1", n), ALU.add))
                        norm(Y, Y, span)
                        link(v.tensor_tensor(y, y, vec("gamma1", n), ALU.mult))
                        link(v.tensor_tensor(y, y, vec("beta1", n), ALU.add))
                    if i == 3:
                        link(v.tensor_tensor(y, y, vec("bias2", n), ALU.add))
                        norm(Y, Y, span)
                        link(v.tensor_tensor(y, y, vec("g2", n), ALU.mult))
                        link(v.tensor_tensor(y, y, vec("b2", n), ALU.add))
                        link(v.tensor_scalar_max(y, y, 0.0))
                    if i in (1, 2, 3):
                        link(v.tensor_tensor(y, y, xN[:, s, :], ALU.add))
                        norm(xN, Y, span)
                if i == 4:
                    def pull(base):
                        for c in range(NC):
                            n = min(4, K - 4 * c)
                            v.wait_ge(turned, base + c + 1)
                            v.tensor_copy(xT[0:D, c * 4 * P:(c * 4 + n) * P], psX[(base + c) % 2][0:D, 0:n * P]).then_inc(copied, 1)
                    link(v.memset(xT[D:D + 1, :], 1.0))
                    pull(0)
                    v.wait_ge(rooted, 1)
                    link(v.tensor_scalar(gb[:, 0:D], gb[:, 0:D], 0.5, 1.0, ALU.mult, ALU.add))
                    link(v.tensor_copy(gb[:, D:2 * D], psF[:, D:2 * D]))

                    def take_out(k, s):
                        v.wait_ge(proj, k + 2)
                        v.tensor_copy(Q[:, bass.ds(k, 1), :], psP[s][:, 0:D].rearrange("p (a f) -> p a f", a=1)).then_inc(took, 1)
                    each(v, K, take_out)
                    v.wait_ge(took, K)
                    link(v.tensor_tensor(Y[:, :, :], Q[:, :, :], vec("bo3"), ALU.add))
                    link(v.tensor_tensor(Y[:, :, :], Y[:, :, :], over(gb[:, 0:D], 1, full), ALU.mult))
                    link(v.tensor_tensor(Y[:, :, :], Y[:, :, :], over(gb[:, D:2 * D], 1, full), ALU.add))
                    link(v.tensor_tensor(Y[:, :, :], Y[:, :, :], xN[:, :, :], ALU.add))
                    norm(x1, Y)
                    link(v.tensor_tensor(x1[:, :, :], x1[:, :, :], vec("ln1g"), ALU.mult))
                    link(v.tensor_tensor(x1[:, :, :], x1[:, :, :], vec("ln1b"), ALU.add))
                    v.sem_inc(asked, 1)
                    pull(NC)

                    def take_ffn(k, s):
                        v.wait_ge(proj, k + K + 2)
                        v.tensor_copy(Q[:, bass.ds(k, 1), :], psP[s][:, 0:D].rearrange("p (a f) -> p a f", a=1)).then_inc(took, 1)
                    each(v, K, take_ffn)
                    v.wait_ge(took, 2 * K)
                    link(v.tensor_tensor(Y[:, :, :], Q[:, :, :], vec("b2v"), ALU.add))
                    link(v.tensor_tensor(Y[:, :, :], Y[:, :, :], x1[:, :, :], ALU.add))
                    norm(Y, Y)
                    link(v.tensor_tensor(Y[:, :, :], Y[:, :, :], vec("ln2g"), ALU.mult))
                    link(v.tensor_tensor(Y[:, :, :], Y[:, :, :], vec("ln2b"), ALU.add))
                    link(v.tensor_tensor(Y[:, :, :], Y[:, :, :], xN[:, :, :], ALU.add))
                    norm(xN, Y)


def store(nc, m, out):
    with ExitStack() as ctx:
        kept = stage_sem(nc, ctx, "kept")
        with nc.Block() as block:
            @block.sync
            def _(sp):
                sp.dma_start(out[0:(P - 1) * K, :].rearrange("(p k) f -> p k f", k=K), m["xN"][0:P - 1, :, :]).then_inc(kept, 16)
                sp.dma_start(out[(P - 1) * K:N, :].rearrange("(p k) f -> p k f", p=1), m["xN"][P - 1:P, 0:LASTN, :]).then_inc(kept, 16)
                sp.wait_ge(kept, 32)


def kernel(**inp):
    import numpy as np
    import concourse.bacc as bacc
    from concourse.bass_utils import run_bass_kernel_spmd as run

    a = {k: np.asarray(v) for k, v in inp.items()}
    pad = TILES * P - E

    def tiled(v, fill):
        return np.concatenate([v, np.full((pad,), fill, v.dtype)]).reshape(TILES, P).T

    def aug(w, b):
        return np.concatenate([w, b[None, :]], axis=0)

    end = np.full((1,), -1, a["dst"].dtype)
    line = np.concatenate([end, a["dst"], np.full((pad,), N, a["dst"].dtype), end])
    arrays = {
        "x": a["x"], "srcT": tiled(a["src"], 0), "typeT": tiled(a["edge_type_8"], 0), "dstT": tiled(a["dst"], N),
        "dstS": np.stack([line[r * L:(r + 1) * L + 2] for r in range(ROWS)]),
        "eaT": np.concatenate([a["edge_attr_64"], np.zeros((pad, D), np.float32)]).T,
        "Wl1": aug(a["L0_gnn_Wl1"].T, a["L0_gnn_bl1"]), "Wr1": aug(a["L0_gnn_Wr1"].T, a["L0_gnn_br1"]),
        "Wl2": aug(a["L0_gnn_Wl2"].T, a["L0_gnn_bl2"]), "Wr2": aug(a["L0_gnn_Wr2"].T, a["L0_gnn_br2"]),
        "Wskip": aug(a["L0_gnn_Wskip"].T, a["L0_gnn_bskip"]),
        "We1": a["L0_gnn_We1"].T, "We2": a["L0_gnn_We2"].T,
        "gatW": a["L1_gnn_W"], "gatWT": a["L1_gnn_W"].T,
        "Wrel": a["L2_gnn_W_r"].transpose(1, 0, 2).reshape(D, REL * D), "Wk": a["L2_gnn_Wk_w"],
        "Wq2": aug(a["L2_gnn_Wq_w"], a["L2_gnn_Wq_bias"]), "Wq2T": aug(a["L2_gnn_Wq_w"], a["L2_gnn_Wq_bias"]).T,
        "bk2": a["L2_gnn_Wk_bias"], "ruleids": a["L2_gnn_rule_ids"], "ruleemb": a["L2_gnn_rule_emb"],
        "Wk3": a["L3_gnn_Wk"], "Wv3": a["L3_gnn_Wv"], "Wq3": aug(a["L3_gnn_Wq"], a["L3_gnn_bq"]),
        "bk3": a["L3_gnn_bk"], "bv3": a["L3_gnn_bv"], "ek": a["L3_gnn_ek_tab"], "ev": a["L3_gnn_ev_tab"],
        "es": a["L3_gnn_es_tab"], "eg": a["L3_gnn_eg_tab"], "Wo3": a["L3_gnn_Wo"],
        "W1": aug(a["L3_gnn_W1"], a["L3_gnn_b1"]), "W2": a["L3_gnn_W2"], "Wf": aug(a["L3_gnn_Wf"], a["L3_gnn_bf"]),
        "task": np.broadcast_to(np.concatenate([a["L3_gnn_task_embedding"], np.ones((1,), np.float32)])[:, None], (D + 1, P)),
    }
    att = np.zeros((D, 8), np.float32)
    for h in range(4):
        att[h * 16:(h + 1) * 16, h] = a["L1_gnn_att_src"][h]
        att[h * 16:(h + 1) * 16, 4 + h] = a["L1_gnn_att_dst"][h]
    arrays["gatAtt"] = att
    vec = {"att1": "L0_gnn_att1", "bo1": "L0_gnn_bo1", "att2": "L0_gnn_att2", "bo2": "L0_gnn_bo2", "bias1": "L1_gnn_bias",
           "gamma1": "L1_gnn_gamma", "beta1": "L1_gnn_beta", "bias2": "L2_gnn_bias", "g2": "L2_gnn_ln_g", "b2": "L2_gnn_ln_b",
           "bo3": "L3_gnn_bo", "ln1g": "L3_gnn_ln1_g", "ln1b": "L3_gnn_ln1_b",
           "b2v": "L3_gnn_b2", "ln2g": "L3_gnn_ln2_g", "ln2b": "L3_gnn_ln2_b"}
    arrays["vec"] = np.broadcast_to(np.stack([a[vec[n]] for n in VECS])[None], (P, len(VECS), D))

    nc = bacc.Bacc("TRN2", target_bir_lowering=False, num_devices=1)
    fed, t = {}, {}
    for name, v in arrays.items():
        v = np.ascontiguousarray(v)
        fed[f"in_{name}"] = v
        t[name] = nc.dram_tensor(f"in_{name}", v.shape, mybir.dt.from_np(v.dtype), kind="ExternalInput").ap()
    out = nc.dram_tensor("out_0", (N, D), F32, kind="ExternalOutput").ap()
    build(nc, t, out)
    r = run(nc, [fed], core_ids=[0])
    return r.results[0]["out_0"]
```
